# Optimizing a Trainium2 kernel written in Bass

```python
import numpy as np
import jax
import jax.numpy as jnp

def _softmax(x, axis=-1):
    return jax.nn.softmax(x, axis=axis)

def _gelu(x):
    return jax.nn.gelu(x, approximate=True)

def _silu(x):
    return jax.nn.silu(x)

def _sigmoid(x):
    return jax.nn.sigmoid(x)

def _layernorm(x, axis=-1, eps=1e-05):
    m = jnp.mean(x, axis=axis, keepdims=True)
    v = jnp.var(x, axis=axis, keepdims=True)
    return (x - m) / jnp.sqrt(v + eps)

def _scatter_add(tgt, idx, src, axis=0):
    return tgt.at[idx].add(src)

def _segment_sum(src, seg, n):
    return jax.ops.segment_sum(src, seg, n)
kernel_name = 'mk_hybrid_d1_jaxref_r8_f080b5'

def setup_inputs(seed: int=0):
    np.random.seed(seed)
    _w = jnp.asarray

    def _L0_attn_a_setup():
        import jax, jax.numpy as jnp
        import numpy as np
        EMB, KDIM, B, S = (128, 64, 8, 256)
        key = jax.random.key(seed)
        kx, kq, kk, kv1, kv2 = jax.random.split(key, 5)

        def xavier(k, shape):
            fan_in, fan_out = shape
            lim = (6.0 / (fan_in + fan_out)) ** 0.5
            return jax.random.uniform(k, shape, jnp.float32, -lim, lim)
        return {'x': jax.random.normal(kx, (B, S, EMB), jnp.float32), 'w_q': xavier(kq, (EMB, KDIM)), 'w_k': xavier(kk, (EMB, KDIM)), 'w_v1': xavier(kv1, (EMB, KDIM)), 'w_v2': xavier(kv2, (KDIM, EMB))}
    _L0_attn_a_in = _L0_attn_a_setup()

    def _L0_attn_b_setup():
        import math
        import jax, jax.numpy as jnp
        import numpy as np
        B, C, D = (4, 256, 128)
        DQ = DV = 64
        H = 16
        key = jax.random.key(seed)
        kx, kq, kk, kv, kw = jax.random.split(key, 5)
        x = jax.random.normal(kx, (B, C, D), dtype=jnp.float32)
        Q = jax.random.normal(kq, (DQ, D, H), dtype=jnp.float32) / math.sqrt(D)
        K = jax.random.normal(kk, (DQ, D, H), dtype=jnp.float32) / math.sqrt(D)
        V = jax.random.normal(kv, (DV, D, H), dtype=jnp.float32) / math.sqrt(D)
        W = jax.random.normal(kw, (D, DV, H), dtype=jnp.float32) / math.sqrt(DV)
        return {'x': x, 'Q': Q, 'K': K, 'V': V, 'W': W}
    _L0_attn_b_in = _L0_attn_b_setup()

    def _L0_ffn_setup():
        import jax, jax.numpy as jnp
        import numpy as np
        TOP_K = 2
        key = jax.random.key(seed)
        ks = jax.random.split(key, 5)
        B, S, D, H, E = (2, 256, 128, 352, 8)
        x = jax.random.normal(ks[0], (B, S, D), dtype=jnp.float32)
        Wg = jax.random.normal(ks[1], (E, D), dtype=jnp.float32) * 0.02
        W1 = jax.random.normal(ks[2], (E, H, D), dtype=jnp.float32) * 0.02
        W2 = jax.random.normal(ks[3], (E, H, D), dtype=jnp.float32) * 0.02
        W3 = jax.random.normal(ks[4], (E, D, H), dtype=jnp.float32) * 0.02
        return {'x': x, 'Wg': Wg, 'W1': W1, 'W2': W2, 'W3': W3}
    _L0_ffn_in = _L0_ffn_setup()
    _d = {'L0_attn_a_x': _L0_attn_a_in['x'], 'L0_attn_a_w_q': _L0_attn_a_in['w_q'], 'L0_attn_a_w_k': _L0_attn_a_in['w_k'], 'L0_attn_a_w_v1': _L0_attn_a_in['w_v1'], 'L0_attn_a_w_v2': _L0_attn_a_in['w_v2'], 'L0_attn_b_Q': _L0_attn_b_in['Q'], 'L0_attn_b_K': _L0_attn_b_in['K'], 'L0_attn_b_V': _L0_attn_b_in['V'], 'L0_attn_b_W': _L0_attn_b_in['W'], 'L0_ffn_Wg': _L0_ffn_in['Wg'], 'L0_ffn_W1': _L0_ffn_in['W1'], 'L0_ffn_W2': _L0_ffn_in['W2'], 'L0_ffn_W3': _L0_ffn_in['W3']}
    _x0 = _d['L0_attn_a_x']
    _d['L0_attn_a_x'] = jax.random.normal(jax.random.fold_in(jax.random.key(seed), 1), (8, 512, 128), dtype=_x0.dtype)
    del _x0
    return _d

def reference(L0_attn_a_x, L0_attn_a_w_q, L0_attn_a_w_k, L0_attn_a_w_v1, L0_attn_a_w_v2, L0_attn_b_Q, L0_attn_b_K, L0_attn_b_V, L0_attn_b_W, L0_ffn_Wg, L0_ffn_W1, L0_ffn_W2, L0_ffn_W3):

    def _L0_attn_a_ref(x, w_q, w_k, w_v1, w_v2):
        import jax, jax.numpy as jnp
        import numpy as np
        EMB, KDIM, B, S = (128, 64, 8, 256)
        seq = x.shape[1]
        queries = jnp.einsum('bse,ek->bsk', x, w_q)
        keys = jnp.einsum('bse,ek->bsk', x, w_k)
        scale = w_q.shape[1] ** (-0.5)
        scores = jnp.einsum('bqk,bsk->bqs', queries, keys) * scale
        causal = jnp.tril(jnp.ones((seq, seq), dtype=bool))
        scores = jnp.where(causal[None, :, :], scores, -jnp.inf)
        attn = jax.nn.softmax(scores, axis=-1)
        values = jnp.einsum('bsk,ke->bse', jnp.einsum('bse,ek->bsk', x, w_v1), w_v2)
        return jnp.einsum('bqs,bse->bqe', attn, values)

    def _L0_attn_b_ref(x, Q, K, V, W):
        import math
        import jax, jax.numpy as jnp
        import numpy as np
        B, C, D = (4, 256, 128)
        DQ = DV = 64
        H = 16
        d_query, d_embed, num_heads = Q.shape
        d_value = V.shape[0]
        sq = math.sqrt(d_query / d_embed)
        sv = math.sqrt(d_value / d_embed)
        q = jnp.einsum('qdh,bcd->bhcq', Q, x) * sq
        k = jnp.einsum('qdh,bcd->bhcq', K, x) * sq
        v = jnp.einsum('vdh,bcd->bhcv', V, x) * sv
        att = jnp.einsum('bhcq,bhCq->bhcC', q, k) / d_query
        T = x.shape[1]
        causal = jnp.arange(T)[:, None] >= jnp.arange(T)[None, :]
        att = jnp.where(causal, att, -jnp.inf)
        p = jax.nn.softmax(att, axis=-1)
        y = jnp.einsum('bhcC,bhCv->bhcv', p, v)
        z = jnp.einsum('dvh,bhcv->bcd', W, y) * (math.sqrt(d_embed / d_value) / num_heads)
        return z

    def _L0_ffn_ref(x, Wg, W1, W2, W3):
        import jax, jax.numpy as jnp
        import numpy as np
        TOP_K = 2
        B, S, D = x.shape
        E = Wg.shape[0]
        xt = x.reshape(B * S, D)
        scores = xt @ Wg.T
        topk_scores, topk_idx = jax.lax.top_k(scores, TOP_K)
        gate = jax.nn.silu(jnp.einsum('td,ehd->teh', xt, W1))
        up = jnp.einsum('td,ehd->teh', xt, W2)
        y = jnp.einsum('teh,edh->ted', gate * up, W3)
        onehot = jax.nn.one_hot(topk_idx, E, dtype=x.dtype)
        w = jnp.einsum('tke,tk->te', onehot, topk_scores)
        out = jnp.einsum('te,ted->td', w, y)
        return out.reshape(B, S, D)
    x = L0_attn_a_x
    x = x + _L0_attn_a_ref(_layernorm(x, axis=-1), L0_attn_a_w_q, L0_attn_a_w_k, L0_attn_a_w_v1, L0_attn_a_w_v2)
    x = x + _L0_ffn_ref(_layernorm(x, axis=-1), L0_ffn_Wg, L0_ffn_W1, L0_ffn_W2, L0_ffn_W3)
    x = x + _L0_attn_b_ref(_layernorm(x, axis=-1), L0_attn_b_Q, L0_attn_b_K, L0_attn_b_V, L0_attn_b_W)
    x = x + _L0_ffn_ref(_layernorm(x, axis=-1), L0_ffn_Wg, L0_ffn_W1, L0_ffn_W2, L0_ffn_W3)
    return x

_drawn_inputs = setup_inputs


def setup_inputs(seed=0):
    import zlib

    import numpy as np

    out = dict(_drawn_inputs(seed))
    spreads = {}
    factors = {'L0_attn_b_Q': 8.0,
     'L0_attn_b_K': 8.0,
     'L0_ffn_Wg': 7.452,
     'L0_ffn_W1': 6.702,
     'L0_ffn_W2': 6.659,
     'L0_ffn_W3': 6.679}
    for name, (base, spread) in spreads.items():
        noise = np.random.default_rng([zlib.crc32(name.encode()), seed]).standard_normal(out[name].shape)
        drawn = base * np.exp(spread * noise) if base else spread * noise
        out[name] = jnp.asarray(drawn.astype(out[name].dtype))
    for name, factor in factors.items():
        out[name] = (out[name] * factor).astype(out[name].dtype)
    return out
```

```python
import concourse.bass as bass
from concourse import mybir
from contextlib import ExitStack

F32 = mybir.dt.float32
F32R = mybir.dt.float32r
BF16 = mybir.dt.bfloat16
ALU = mybir.AluOpType
ACT = mybir.ActivationFunctionType
AX = mybir.AxisListType

P = 128
NB, T, D = 8, 512, 128
QT = T // P
KD = 64
NH = 16
NP = NH // 2
NE, EH = 8, 352
NC = 3
EC = NE * NC
LAST = EH - 2 * P
EHP = 2848
EPS = 1e-5
MASKED = -3.0e38

P_AT = [0, 128, 384, 768]
PT_AT = {0: 0, 1: 512, 3: 896, 2: 1024}
PT_BANKS = [((0,), 0, 512), ((1, 3), 512, 512), ((2,), 1024, 256)]
NPT = 1280


def live(b):
    return not isinstance(b, int) or 0 <= b < NB


def wait(eng, sem, value):
    if not isinstance(value, int) or value > 0:
        eng.wait_ge(sem, value)


def wait_apart(nc, dve, g, sem, value):
    wait(dve, sem, value)
    if not isinstance(value, int):
        nc.vector.memset(g.unused[:], 0.0)


def tokens(b):
    return bass.ds(b * T, T)


def tile(b, t):
    return b * QT + t


def three_passes(nc, out, st, mv, start, stop):
    nc.tensor.matmul(out, st[0], mv[0], start=start, stop=False)
    nc.tensor.matmul(out, st[0], mv[1], start=False, stop=False)
    return nc.tensor.matmul(out, st[1], mv[0], start=False, stop=stop)


class Shared:
    pass


def each_sequence(eng, body):
    body(0)
    body(1)
    with eng.Fori(2, NB) as b:
        body(b)
    body(NB)



class Norm:

    def __init__(self, nc, ctx, name, xn=None):
        sb = lambda n, s, d: ctx.enter_context(nc.sbuf_tensor(f"{name}_{n}", s, d))
        sem = lambda n: ctx.enter_context(nc.semaphore(f"{name}_{n}"))
        self.stats = sb("stats", [P, QT, 6], F32)
        self.mv = sb("mv", [P, QT, 2], F32)
        self.veps = sb("veps", [P, QT], F32)
        self.rstd = sb("rstd", [P, QT], F32)
        self.xn = sb("xn", [P, T], F32) if xn is None else xn
        self.stats_done = sem("stats_done")
        self.mv_done = sem("mv_done")
        self.veps_done = sem("veps_done")
        self.rstd_done = sem("rstd_done")
        self.xn_done = sem("xn_done")
        self.xnt_full = sem("xnt_full")
        self.hi_done = sem("hi_done")
        self.lo_done = sem("lo_done")


def norm_stats(nc, dve, g, n, b):
    for t in range(QT):
        nc.vector.bn_stats(n.stats[:, t, :], g.x_tok[:, tile(b, t), :]).then_inc(n.stats_done, 1)
    wait(dve, n.rstd_done, b)
    wait_apart(nc, dve, g, n.stats_done, b * QT + QT)
    for t in range(QT):
        nc.vector.bn_aggr(n.mv[:, t, :], n.stats[:, t, :]).then_inc(n.mv_done, 1)


def norm_rstd(nc, pool, g, n, b):
    wait(pool, n.xn_done, b * QT)
    pool.wait_ge(n.mv_done, b * QT + QT)
    nc.gpsimd.tensor_tensor(n.veps[:], n.mv[:, :, 1], g.eps[:], ALU.add).then_inc(n.veps_done, 1)
    pool.wait_ge(n.veps_done, b + 1)
    nc.gpsimd.tensor_tensor(n.rstd[:], n.veps[:], g.minus_half[:], ALU.pow).then_inc(n.rstd_done, 1)


def norm_apply(nc, dve, g, n, b):
    dve.wait_ge(n.rstd_done, b + 1)
    dve.wait_ge(n.mv_done, b * QT + QT)
    wait(dve, n.xnt_full, b)
    for t in range(QT):
        nc.vector.tensor_scalar(n.xn[:, t * D:t * D + D], g.x_tok[:, tile(b, t), :], n.mv[:, t, 0:1], n.rstd[:, t:t + 1],
                                ALU.subtract, ALU.mult).then_inc(n.xn_done, 1)


def norm_transpose(nc, pe, g, n, b, bank):
    pe.wait_ge(n.xn_done, b * QT + QT)
    for t in range(QT):
        last = nc.tensor.transpose(bank[:, t * P:t * P + P], n.xn[:, t * D:t * D + D], g.ident[:])
    last.then_inc(n.xnt_full, 1)


def norm_hi(nc, act, g, n, b, bank):
    act.wait_ge(n.xnt_full, b + 1)
    nc.scalar.activation(g.xn_hi[:, tokens(b)], bank[:], ACT.Copy).then_inc(n.hi_done, 1)


def norm_lo(nc, dve, g, n, b, bank):
    dve.wait_ge(n.hi_done, b + 1)
    nc.vector.tensor_tensor(g.xn_lo[:, tokens(b)], bank[:], g.xn_hi[:, tokens(b)].bitcast(F32),
                            ALU.subtract).then_inc(n.lo_done, 1)



def prepare(nc, g, ins):
    x, w_q, w_k, w_v1, w_v2, Q, K, V, W, Wg, W1, W2, W3 = ins
    with ExitStack() as ctx:
        sb = lambda n, s, d: ctx.enter_context(nc.sbuf_tensor(n, s, d))
        pb = lambda n: ctx.enter_context(nc.psum_tensor(n, [P, 512], F32))
        sem = lambda n: ctx.enter_context(nc.semaphore(n))
        n = Norm(nc, ctx, "n0")
        a_raw = sb("a_raw", [P, 3, P], F32)
        v2_raw = sb("v2_raw", [KD, P], F32)
        wg_raw = sb("wg_raw", [NE, D], F32)
        f_raw = [sb(f"f_raw{i}", [P, EHP], F32) for i in range(2)]
        w3_raw = f_raw[0]
        qkv_raw = [sb(f"qkv_raw{i}", [P, KD, NH], F32) for i in range(4)]
        w_perm = sb("w_perm", [P, NH * KD], F32)
        norm_bank = [pb(f"norm_bank{i}") for i in range(2)]
        bank = [pb(f"prep_bank{i}") for i in range(4)]
        x_in = [sem(f"x_in{b}") for b in range(NB)]
        a_in = sem("a_in")
        wg_in = sem("wg_in")
        f_in = [sem(f"f_in{i}") for i in range(3)]
        b_in = [sem(f"b_in{i}") for i in range(4)]
        zeroed = sem("zeroed")
        consts = sem("consts")
        direct_hi = sem("direct_hi")
        direct_lo = sem("direct_lo")
        perm_done = sem("perm_done")
        turned = sem("turned")
        turned_hi = sem("turned_hi")
        turned_lo = sem("turned_lo")

        direct = [
            (a_raw[:, 0, :], KD ** -0.5, g.a_wq[0][:], g.a_wq[1][:], a_in, 96),
            (a_raw[:, 1, :], 1.0, g.a_wk[0][:], g.a_wk[1][:], a_in, 96),
            (a_raw[:, 2, 0:KD], 1.0, g.a_wv1[0][:], g.a_wv1[1][:], a_in, 96),
            (v2_raw[:], 1.0, g.a_wv2[0][:], g.a_wv2[1][:], a_in, 96),
        ]
        for i, (parts, scale) in enumerate(((g.b_q, 1.0 / 128), (g.b_k, 1.0), (g.b_v, 1.0))):
            raw = qkv_raw[i][:].rearrange("p q h -> p h q")
            hi, lo = (part[:].rearrange("p (h q) -> p h q", h=NH) for part in parts)
            direct.append((raw, scale, hi, lo, b_in[i], 16))

        groups = [([(wg_raw[:], g.ident[0:NE, 0:NE], NE)], wg_in, 16,
                   g.wg[0][:, 0:NE], g.wg[1][:, 0:NE])]
        for i, parts in enumerate((g.w1, g.w2)):
            for j in range(0, 22, 4):
                m = min(4, 22 - j)
                groups.append(([(f_raw[i][:, (j + k) * P:(j + k) * P + P], g.ident[:], P) for k in range(m)], f_in[i], 16,
                               parts[0][:, j * P:(j + m) * P], parts[1][:, j * P:(j + m) * P]))
        for c in range(0, EC, 4):
            at = [(c + k) // NC * EH + (c + k) % NC * P for k in range(4)]
            groups.append(([(w3_raw[:, a:a + P], g.ident[:], P) for a in at], f_in[2], 16,
                           g.w3[0][:, c * P:(c + 4) * P], g.w3[1][:, c * P:(c + 4) * P]))
        for p in range(0, NP, 4):
            groups.append(([(w_perm[:, (p + k) * P:(p + k) * P + P], g.ident[:], P) for k in range(4)],
                           perm_done, 1, g.b_w[0][:, p * P:(p + 4) * P], g.b_w[1][:, p * P:(p + 4) * P]))

        block = ctx.enter_context(nc.Block())

        @block.sync
        def _(sp):
            for b in range(NB):
                sp.dma_start(g.x_tok[:, b * QT:b * QT + QT, :],
                             x[b].rearrange("(t p) d -> p t d", p=P)).then_inc(x_in[b], 16)
                if b == 0:
                    for k in range(2):
                        sp.dma_start(a_raw[:, 0, k * KD:k * KD + KD], w_q).then_inc(a_in, 16)
                        sp.dma_start(a_raw[:, 1, k * KD:k * KD + KD], w_k).then_inc(a_in, 16)
                    sp.dma_start(a_raw[:, 2, 0:KD], w_v1).then_inc(a_in, 16)
                    sp.dma_start(v2_raw[:], w_v2).then_inc(a_in, 16)
            sp.dma_start(wg_raw[:], Wg).then_inc(wg_in, 16)
            for i, w in enumerate((W1, W2)):
                flat = w.rearrange("e h d -> (e h) d").rearrange("(j p) d -> p j d", p=P)
                sp.dma_start(f_raw[i][:, 0:NE * EH].rearrange("p (j d) -> p j d", d=D), flat).then_inc(f_in[i], 16)
            for i, w in enumerate((Q, K, V)):
                sp.dma_start(qkv_raw[i][:], w.rearrange("q d h -> d q h")).then_inc(b_in[i], 16)
            sp.dma_start(qkv_raw[3][:], W).then_inc(b_in[3], 16)
            sp.wait_ge(turned, 7)
            sp.dma_start(w3_raw[:, 0:NE * EH].rearrange("p (e h) -> p e h", e=NE),
                         W3.rearrange("e d h -> d e h")).then_inc(f_in[2], 16)

        @block.gpsimd
        def _(pool):
            nc.gpsimd.memset(g.ident[:], 0.0).then_inc(zeroed, 1)
            nc.gpsimd.memset(g.ident_bf[:], 0.0).then_inc(zeroed, 1)
            nc.gpsimd.memset(g.mask[:], 0.0).then_inc(zeroed, 1)
            nc.gpsimd.memset(g.earlier[:], 0.0).then_inc(zeroed, 1)
            nc.gpsimd.memset(g.minus_half[:], -0.5).then_inc(consts, 1)
            nc.gpsimd.memset(g.eps[:], EPS).then_inc(consts, 1)
            for part in g.wg:
                nc.gpsimd.memset(part[:].bitcast(F32), 0.0).then_inc(consts, 1)
            nc.gpsimd.memset(w3_raw[:, NE * EH:EHP], 0.0).then_inc(consts, 1)
            for part in g.w1 + g.w2:
                nc.gpsimd.memset(part[:, NE * EH:EHP].bitcast(F32), 0.0).then_inc(consts, 1)
            pool.wait_ge(zeroed, 4)
            for idn in (g.ident, g.ident_bf):
                nc.gpsimd.affine_select(out=idn[:], in_=idn[:], compare_op=ALU.not_equal, fill=1.0, base=0,
                                        pattern=[[-1, P]], channel_multiplier=1).then_inc(consts, 1)
            nc.gpsimd.affine_select(out=g.mask[:], in_=g.mask[:], compare_op=ALU.is_ge, fill=MASKED, base=0,
                                    pattern=[[-1, P]], channel_multiplier=1).then_inc(consts, 1)
            nc.gpsimd.affine_select(out=g.earlier[:], in_=g.earlier[:], compare_op=ALU.is_ge, fill=1.0, base=0,
                                    pattern=[[-1, NE], [1, NE]], channel_multiplier=0).then_inc(consts, 1)
            pool.wait_ge(consts, 13)
            norm_rstd(nc, pool, g, n, 0)
            with pool.Fori(1, NB) as b:
                norm_rstd(nc, pool, g, n, b)

        @block.vector
        def _(dve):
            dve.wait_ge(consts, 13)
            for i in range(4):
                raw, scale, hi, lo, loaded, count = direct[i]
                dve.wait_ge(direct_hi, i + 1)
                nc.vector.scalar_tensor_tensor(lo, raw, scale, hi.bitcast(F32), ALU.mult,
                                               ALU.subtract).then_inc(direct_lo, 1)
            for b in range(NB):
                dve.wait_ge(x_in[b], 16)
            norm_stats(nc, dve, g, n, 0)
            norm_apply(nc, dve, g, n, 0)
            with dve.Fori(1, NB) as b:
                norm_stats(nc, dve, g, n, b)
                norm_lo(nc, dve, g, n, b - 1, norm_bank[0])
                norm_apply(nc, dve, g, n, b)
            norm_lo(nc, dve, g, n, NB - 1, norm_bank[0])
            dve.wait_ge(b_in[3], 16)
            nc.vector.tensor_scalar(w_perm[:].rearrange("p (h v) -> p h v", h=NH), qkv_raw[3][:].rearrange("p v h -> p h v"), 1.0 / NH, None,
                                    ALU.mult).then_inc(perm_done, 1)
            for i in range(4, len(direct)):
                raw, scale, hi, lo, loaded, count = direct[i]
                dve.wait_ge(direct_hi, i + 1)
                nc.vector.scalar_tensor_tensor(lo, raw, scale, hi.bitcast(F32), ALU.mult,
                                               ALU.subtract).then_inc(direct_lo, 1)
            for i, (tiles, loaded, count, hi, lo) in enumerate(groups):
                dve.wait_ge(turned_hi, i + 1)
                nc.vector.tensor_tensor(lo, bank[i % 4][:, 0:len(tiles) * tiles[0][2]], hi.bitcast(F32),
                                        ALU.subtract).then_inc(turned_lo, 1)

        @block.scalar
        def _(act):
            act.wait_ge(consts, 13)
            for i in range(4):
                raw, scale, hi, lo, loaded, count = direct[i]
                act.wait_ge(loaded, count)
                nc.scalar.activation(hi, raw, ACT.Copy, scale=scale).then_inc(direct_hi, 1)
            with act.Fori(0, NB) as b:
                norm_hi(nc, act, g, n, b, norm_bank[0])
            for i in range(4, len(direct)):
                raw, scale, hi, lo, loaded, count = direct[i]
                act.wait_ge(loaded, count)
                nc.scalar.activation(hi, raw, ACT.Copy, scale=scale).then_inc(direct_hi, 1)
            for i, (tiles, loaded, count, hi, lo) in enumerate(groups):
                act.wait_ge(turned, i + 1)
                nc.scalar.activation(hi, bank[i % 4][:, 0:len(tiles) * tiles[0][2]], ACT.Copy).then_inc(turned_hi, 1)

        @block.tensor
        def _(pe):
            pe.wait_ge(consts, 13)
            norm_transpose(nc, pe, g, n, 0, norm_bank[0])
            with pe.Fori(1, NB) as b:
                pe.wait_ge(n.lo_done, b)
                norm_transpose(nc, pe, g, n, b, norm_bank[0])
            for i, (tiles, loaded, count, hi, lo) in enumerate(groups):
                pe.wait_ge(loaded, count)
                wait(pe, turned_lo, i - 3)
                for k, (src, ident, width) in enumerate(tiles):
                    last = nc.tensor.transpose(bank[i % 4][:, k * width:k * width + width], src, ident)
                last.then_inc(turned, 1)



class Head:

    def __init__(self, nc, ctx, name, g, probs, v_cols):
        sb = lambda n, s, d: ctx.enter_context(nc.sbuf_tensor(f"{name}_{n}", s, d))
        pb = lambda n: ctx.enter_context(nc.psum_tensor(f"{name}_{n}", [P, 512], F32))
        sem = lambda n: ctx.enter_context(nc.semaphore(f"{name}_{n}"))
        self.ident, self.ident_bf, self.mask = g.ident, g.ident_bf, g.mask
        self.probs = [sb(f"probs{i}", [P, NPT], F32) for i in range(probs)]
        self.pt = (sb("pt_hi", [P, NPT], F32R), sb("pt_lo", [P, NPT], F32R))
        self.neg_max = sb("neg_max", [P, QT], F32)
        self.sums = sb("sums", [P, QT], F32)
        self.recip = sb("recip", [P, QT], F32)
        self.v = sb("v", [P, v_cols], F32R)
        self.y = sb("y", [P, T], F32)
        self.y_parts = (sb("y_hi", [P, T], F32R), sb("y_lo", [P, T], F32R))
        self.z = sb("z", [P, T], F32)
        self.x_cur = (sb("x_cur_hi", [P, T], F32R), sb("x_cur_lo", [P, T], F32R))
        self.s_bank = [pb(f"s_bank{i}") for i in range(2)]
        self.ring = [pb(f"ring{i}") for i in range(3)]
        self.pv_bank = pb("pv_bank")
        self.z_bank = pb("z_bank")
        self.aux_bank = pb("aux_bank")
        self.filled = sem("filled")
        self.ring_hi = sem("ring_hi")
        self.ring_lo = sem("ring_lo")
        self.s_full = sem("s_full")
        self.max_done = sem("max_done")
        self.exp_done = sem("exp_done")
        self.recip_done = sem("recip_done")
        self.probs_done = sem("probs_done")
        self.pv_full = sem("pv_full")
        self.low_done = sem("low_done")
        self.y_done = sem("y_done")
        self.y_hi_done = sem("y_hi_done")
        self.y_lo_done = sem("y_lo_done")
        self.z_full = sem("z_full")
        self.z_done = sem("z_done")
        self.zt_full = sem("zt_full")
        self.x_done = sem("x_done")
        self.x_cur_in = sem("x_cur_in")


def split_hi(nc, act, hd, r, n, dst, src=lambda bank: bank[:]):
    act.wait_ge(hd.filled, r + 1)
    nc.scalar.activation(dst, src(hd.ring[n % 3]), ACT.Copy).then_inc(hd.ring_hi, 1)


def split_lo(nc, dve, hd, r, n, dst, hi, src=lambda bank: bank[:]):
    dve.wait_ge(hd.ring_hi, r + 1)
    nc.vector.tensor_tensor(dst, src(hd.ring[n % 3]), hi.bitcast(F32), ALU.subtract).then_inc(hd.ring_lo, 1)


def head_transpose(nc, pe, hd, u, probs, r, n):
    pe.wait_ge(hd.probs_done, u * QT + QT)
    for k, (key_tiles, at, width) in enumerate(PT_BANKS):
        wait(pe, hd.ring_lo, r + k - 2)
        for j in key_tiles:
            for i in range(j, QT):
                to = PT_AT[j] - at + (i - j) * P
                last = nc.tensor.transpose(hd.ring[(n + k) % 3][:, to:to + P],
                                           probs[:, P_AT[i] + j * P:P_AT[i] + j * P + P], hd.ident[:])
        last.then_inc(hd.filled, 1)


def head_transposed_hi(nc, act, hd, r, n):
    for k, (_, at, width) in enumerate(PT_BANKS):
        split_hi(nc, act, hd, r + k, n + k, hd.pt[0][:, at:at + width], lambda bank: bank[:, 0:width])


def head_transposed_lo(nc, dve, hd, r, n):
    for k, (_, at, width) in enumerate(PT_BANKS):
        split_lo(nc, dve, hd, r + k, n + k, hd.pt[1][:, at:at + width], hd.pt[0][:, at:at + width],
                 lambda bank: bank[:, 0:width])


def head_mask(nc, hd, i):
    return nc.tensor.matmul(hd.s_bank[i % 2][:, i * P:i * P + P], hd.ident_bf[:], hd.mask[:],
                            start=False, stop=True)


def head_max(nc, dve, hd, u):
    for i in range(QT):
        dve.wait_ge(hd.s_full, u * QT + i + 1)
        nc.vector.tensor_reduce(hd.neg_max[:, i:i + 1], hd.s_bank[i % 2][:, 0:(i + 1) * P], AX.X, ALU.max,
                                negate=True).then_inc(hd.max_done, 1)


def head_exp(nc, act, hd, u, probs):
    wait(act, hd.recip_done, u)
    for i in range(QT):
        act.wait_ge(hd.max_done, u * QT + i + 1)
        nc.scalar.activation(probs[:, P_AT[i]:P_AT[i] + (i + 1) * P], hd.s_bank[i % 2][:, 0:(i + 1) * P],
                             ACT.Exp, bias=hd.neg_max[:, i:i + 1],
                             accum_out=hd.sums[:, i:i + 1]).then_inc(hd.exp_done, 1)


def head_recip(nc, dve, hd, u):
    dve.wait_ge(hd.exp_done, u * QT + QT)
    wait(dve, hd.probs_done, u * QT)
    nc.vector.reciprocal(hd.recip[:], hd.sums[:]).then_inc(hd.recip_done, 1)


def head_probs(nc, pool, hd, u, probs):
    pool.wait_ge(hd.recip_done, u + 1)
    for i in range(QT):
        part = probs[:, P_AT[i]:P_AT[i] + (i + 1) * P]
        nc.gpsimd.tensor_tensor(part, part, hd.recip[:, i:i + 1].to_broadcast([P, (i + 1) * P]),
                                ALU.mult).then_inc(hd.probs_done, 1)


def head_pv(nc, pe, hd, u, r_end, v_at):
    pe.wait_ge(hd.ring_lo, r_end)
    wait(pe, hd.y_done, u)
    for j in range(QT):
        v = hd.v[:, v_at(j):v_at(j) + 2 * KD]
        for part in range(2):
            last = nc.tensor.matmul(hd.pv_bank[:, j * P:T], v, hd.pt[part][:, PT_AT[j]:PT_AT[j] + T - j * P],
                                    start=(j == 0 and part == 0), stop=(j == QT - 1 and part == 1))
    last.then_inc(hd.pv_full, 1)


def head_low(nc, act, hd, u, row, split):
    act.wait_ge(hd.pv_full, u + 1)
    wait(act, hd.y_lo_done, split)
    nc.scalar.activation(hd.y[row:row + KD, :], hd.pv_bank[KD:P, :], ACT.Copy).then_inc(hd.low_done, 1)


def head_y(nc, dve, hd, u, row):
    dve.wait_ge(hd.low_done, u + 1)
    y = hd.y[row:row + KD, :]
    nc.vector.tensor_tensor(y, hd.pv_bank[0:KD, :], y, ALU.add).then_inc(hd.y_done, 1)


def output_copy(nc, act, hd, b):
    act.wait_ge(hd.z_full, b + 1)
    nc.scalar.activation(hd.z[:], hd.z_bank[:], ACT.Copy).then_inc(hd.z_done, 1)


def output_transpose(nc, pe, hd, b):
    pe.wait_ge(hd.z_done, b + 1)
    for t in range(QT):
        last = nc.tensor.transpose(hd.aux_bank[:, t * P:t * P + P], hd.z[:, t * P:t * P + P], hd.ident[:])
    last.then_inc(hd.zt_full, 1)


def output_add(nc, dve, g, hd, b):
    dve.wait_ge(hd.zt_full, b + 1)
    rows = g.x_tok[:, bass.ds(b * QT, QT), :]
    nc.vector.tensor_tensor(rows, rows, hd.aux_bank[:].rearrange("p (t d) -> p t d", t=QT),
                            ALU.add).then_inc(hd.x_done, 1)
    wait_apart(nc, dve, g, hd.x_done, b + 1)


def load_x_cur(sp, g, hd, b):
    for part, src in zip(hd.x_cur, (g.xn_hi, g.xn_lo)):
        sp.dma_start(part[:].bitcast(F32), src[:, tokens(b)].bitcast(F32)).then_inc(hd.x_cur_in, 16)



def attention_a(nc, g):
    RA = 6
    with ExitStack() as ctx:
        hd = Head(nc, ctx, "a", g, 1, QT * 2 * KD)
        sb = lambda n, s, d: ctx.enter_context(nc.sbuf_tensor(n, s, d))
        n = Norm(nc, ctx, "n1", hd.z)
        q_stack = sb("q_stack", [P, T], F32R)
        k_twice = (sb("k_twice_hi", [P, T], F32R), sb("k_twice_lo", [P, T], F32R))
        v_parts = [hd.v[:].rearrange("p (t v) -> p t v", t=QT)[:, :, k * KD:k * KD + KD] for k in range(2)]
        v_bank = lambda bank: bank[:, 0:QT * KD].rearrange("p (t v) -> p t v", t=QT)
        block = ctx.enter_context(nc.Block())

        def steps(eng, body):
            for b in range(4):
                body(b)
            with eng.Fori(4, NB) as b:
                body(b)
            for b in range(NB, NB + 4):
                body(b)

        def t_at(b):
            return b * RA + 2

        @block.sync
        def _(sp):
            load_x_cur(sp, g, hd, 0)
            with sp.Fori(1, NB) as b:
                sp.wait_ge(hd.filled, t_at(b - 1) + 4)
                load_x_cur(sp, g, hd, b)

        @block.gpsimd
        def _(pool):
            def body(b):
                if live(b):
                    head_probs(nc, pool, hd, b, hd.probs[0])
                if live(b - 3):
                    norm_rstd(nc, pool, g, n, b - 3)

            steps(pool, body)

        @block.tensor
        def _(pe):
            def body(b):
                if live(b - 4):
                    norm_transpose(nc, pe, g, n, b - 4, hd.aux_bank)
                if live(b - 3):
                    pe.wait_ge(hd.y_lo_done, b - 2)
                    wait(pe, hd.z_done, b - 3)
                    three_passes(nc, hd.z_bank[:], [w[:] for w in g.a_wv2], [y[0:KD, :] for y in hd.y_parts],
                                 True, True).then_inc(hd.z_full, 1)
                if live(b - 2):
                    head_pv(nc, pe, hd, b - 2, t_at(b - 2) + 4, lambda j: j * 2 * KD)
                if live(b - 1):
                    r = t_at(b - 1)
                    head_transpose(nc, pe, hd, b - 1, hd.probs[0], r, 2)
                    pe.wait_ge(hd.ring_lo, r + 1)
                    pe.wait_ge(hd.x_cur_in, b * 32)
                    for t in range(QT):
                        last = three_passes(nc, hd.ring[2][:, t * KD:t * KD + KD],
                                            [x[:, t * P:t * P + P] for x in hd.x_cur],
                                            [g.a_wv1[0][:], g.a_wv1[1][:]], True, True)
                    last.then_inc(hd.filled, 1)
                if live(b):
                    for k, w in enumerate((g.a_wq, g.a_wk)):
                        wait(pe, hd.ring_lo, b * RA + k - 2)
                        three_passes(nc, hd.ring[k][:], [w[0][:], w[1][:]],
                                     [x[:, tokens(b)] for x in (g.xn_hi, g.xn_lo)], True,
                                     True).then_inc(hd.filled, 1)
                if live(b - 3):
                    wait(pe, n.lo_done, b - 3)
                    output_transpose(nc, pe, hd, b - 3)
                if live(b):
                    pe.wait_ge(hd.ring_lo, b * RA + 2)
                    for i in range(QT):
                        wait(pe, hd.exp_done, b * QT + i - 1)
                        keys = (i + 1) * P
                        for part in range(2):
                            nc.tensor.matmul(hd.s_bank[i % 2][:, 0:keys], q_stack[:, i * P:i * P + P],
                                             k_twice[part][:, 0:keys], start=(part == 0), stop=False)
                        head_mask(nc, hd, i).then_inc(hd.s_full, 1)

            steps(pe, body)

        @block.scalar
        def _(act):
            def body(b):
                if live(b - 4):
                    norm_hi(nc, act, g, n, b - 4, hd.aux_bank)
                if live(b - 2):
                    head_low(nc, act, hd, b - 2, 0, b - 2)
                if live(b - 1):
                    head_transposed_hi(nc, act, hd, t_at(b - 1), 2)
                    split_hi(nc, act, hd, t_at(b - 1) + 3, 2, v_parts[0], v_bank)
                if live(b):
                    split_hi(nc, act, hd, b * RA, 0, q_stack[:])
                    split_hi(nc, act, hd, b * RA + 1, 1, k_twice[0][:])
                if live(b - 3):
                    output_copy(nc, act, hd, b - 3)
                if live(b - 2):
                    act.wait_ge(hd.y_done, b - 1)
                    nc.scalar.activation(hd.y_parts[0][0:KD, :], hd.y[0:KD, :], ACT.Copy).then_inc(hd.y_hi_done, 1)
                if live(b):
                    head_exp(nc, act, hd, b, hd.probs[0])

            steps(act, body)

        @block.vector
        def _(dve):
            def body(b):
                if live(b - 4):
                    norm_lo(nc, dve, g, n, b - 4, hd.aux_bank)
                if live(b - 2):
                    head_y(nc, dve, hd, b - 2, 0)
                if live(b - 1):
                    head_transposed_lo(nc, dve, hd, t_at(b - 1), 2)
                    split_lo(nc, dve, hd, t_at(b - 1) + 3, 2, v_parts[1], v_parts[0], v_bank)
                if live(b):
                    dve.wait_ge(hd.ring_hi, b * RA + 1)
                    nc.vector.tensor_tensor(q_stack[KD:P, :], hd.ring[0][KD:P, :], q_stack[KD:P, :].bitcast(F32),
                                            ALU.subtract).then_inc(hd.ring_lo, 1)
                    split_lo(nc, dve, hd, b * RA + 1, 1, k_twice[1][:], k_twice[0][:])
                if live(b - 2):
                    dve.wait_ge(hd.y_hi_done, b - 1)
                    nc.vector.tensor_tensor(hd.y_parts[1][0:KD, :], hd.y[0:KD, :], hd.y_parts[0][0:KD, :].bitcast(F32),
                                            ALU.subtract).then_inc(hd.y_lo_done, 1)
                if live(b):
                    head_max(nc, dve, hd, b)
                    head_recip(nc, dve, hd, b)
                if live(b - 3):
                    output_add(nc, dve, g, hd, b - 3)
                    norm_stats(nc, dve, g, n, b - 3)
                    norm_apply(nc, dve, g, n, b - 3)

            steps(dve, body)



def experts(nc, g, name, out=None):
    with ExitStack() as ctx:
        sb = lambda n, s, d: ctx.enter_context(nc.sbuf_tensor(f"{name}_{n}", s, d))
        pb = lambda n: ctx.enter_context(nc.psum_tensor(f"{name}_{n}", [P, 512], F32))
        sem = lambda n: ctx.enter_context(nc.semaphore(f"{name}_{n}"))
        n = Norm(nc, ctx, f"{name}_n")
        act_gate = [sb(f"act_gate{i}", [P, T], F32) for i in range(2)]
        hidden = [sb(f"hidden{i}", [P, T], F32) for i in range(2)]
        hidden_parts = [(sb(f"hidden_hi{i}", [P, T], F32R), sb(f"hidden_lo{i}", [P, T], F32R)) for i in range(3)]
        y_sb = sb("y_sb", [P, T], F32)
        scores_t = sb("scores_t", [P, T], F32)
        scores = sb("scores", [P, QT * NE], F32)
        better = sb("better", [P, QT * NE, NE], F32)
        equal = sb("equal", [P, QT * NE, NE], F32)
        rank = sb("rank", [P, QT * NE], F32)
        weight = sb("weight", [P, QT * NE], F32)
        gate_bank = [pb(f"gate_bank{i}") for i in range(2)]
        up_bank = [pb(f"up_bank{i}") for i in range(2)]
        y_bank = [pb(f"y_bank{i}") for i in range(2)]
        turn_bank = pb("turn_bank")
        gate_full = sem("gate_full")
        up_full = sem("up_full")
        silu_done = sem("silu_done")
        hidden_done = sem("hidden_done")
        hi_done = sem("hi_done")
        lo_done = sem("lo_done")
        chunk_done = sem("chunk_done")
        y_copied = sem("y_copied")
        y_turned = sem("y_turned")
        added = sem("added")
        sc_full = sem("sc_full")
        sc_copied = sem("sc_copied")
        sc_turned = sem("sc_turned")
        sc_read = sem("sc_read")
        compared = sem("compared")
        weight_done = sem("weight_done")
        stored = sem("stored")
        block = ctx.enter_context(nc.Block())

        def lagging(b, c, lag):
            return (b, c - lag) if c >= lag else (b - 1, c - lag + EC)

        @block.tensor
        def _(pe):
            def turn(b, e):
                pe.wait_ge(y_copied, b * NE + e + 1)
                wait(pe, added, b * NE + e)
                if e == 0:
                    pe.wait_ge(sc_read, b + 1)
                if e == 1 and out is None:
                    wait(pe, n.lo_done, b)
                for t in range(QT):
                    last = nc.tensor.transpose(turn_bank[:, t * P:t * P + P], y_sb[:, t * P:t * P + P], g.ident[:])
                last.then_inc(y_turned, 1)

            def body(b):
                for c in range(EC):
                    m = b * EC + c
                    e, k = divmod(c, NC)
                    if live(b):
                        mv = [x[:, tokens(b)] for x in (g.xn_hi, g.xn_lo)]
                        cols = slice(e * EH + k * P, e * EH + k * P + P)
                        wait(pe, silu_done, m - 1)
                        three_passes(nc, gate_bank[c % 2][:], [w[:, cols] for w in g.w1], mv, True,
                                     True).then_inc(gate_full, 1)
                        wait(pe, hidden_done, m - 1)
                        three_passes(nc, up_bank[c % 2][:], [w[:, cols] for w in g.w2], mv, True,
                                     True).then_inc(up_full, 1)
                        if c == 4:
                            wait(pe, added, b * NE)
                            three_passes(nc, turn_bank[:], [w[:] for w in g.wg], mv, True,
                                         True).then_inc(sc_full, 1)
                        if c == 5:
                            pe.wait_ge(sc_copied, b + 1)
                            for t in range(QT):
                                last = nc.tensor.transpose(turn_bank[:, t * P:t * P + P],
                                                           scores_t[:, t * P:t * P + P], g.ident[:])
                            last.then_inc(sc_turned, 1)
                    if out is None and c == 8 and live(b - 1):
                        pe.wait_ge(added, b * NE + (1 if live(b) else 0))
                        norm_transpose(nc, pe, g, n, b - 1, turn_bank)
                    b6, c6 = lagging(b, c, 6)
                    if c6 % NC == 0 and live(b6):
                        turn(b6, c6 // NC)
                    b2, c2 = lagging(b, c, 2)
                    if live(b2):
                        e2, k2 = divmod(c2, NC)
                        pe.wait_ge(lo_done, m - 1)
                        if k2 == 0:
                            wait(pe, y_copied, b2 * NE + e2 - 1)
                        rows = LAST if k2 == NC - 1 else P
                        st = [w[0:rows, c2 * P:c2 * P + P] for w in g.w3]
                        mv2 = [h[0:rows, :] for h in hidden_parts[c2 % 3]]
                        three_passes(nc, y_bank[e2 % 2][:], st, mv2, k2 == 0, k2 == NC - 1).then_inc(chunk_done, 1)

            each_sequence(pe, body)

        @block.scalar
        def _(act):
            def body(b):
                for c in range(EC):
                    m = b * EC + c
                    if live(b):
                        act.wait_ge(gate_full, m + 1)
                        wait(act, hidden_done, m - 1)
                        nc.scalar.activation(act_gate[c % 2][:], gate_bank[c % 2][:], ACT.Silu).then_inc(silu_done, 1)
                        if c == 4:
                            act.wait_ge(sc_full, b + 1)
                            nc.scalar.activation(scores_t[:], turn_bank[:], ACT.Copy).then_inc(sc_copied, 1)
                    b1, c1 = lagging(b, c, 1)
                    if live(b1):
                        act.wait_ge(hidden_done, m)
                        wait(act, chunk_done, m - 3)
                        nc.scalar.activation(hidden_parts[c1 % 3][0][:], hidden[c1 % 2][:],
                                             ACT.Copy).then_inc(hi_done, 1)
                    b5, c5 = lagging(b, c, 5)
                    if c5 % NC == 0 and live(b5):
                        e5 = c5 // NC
                        act.wait_ge(chunk_done, b5 * EC + c5 + NC)
                        wait(act, y_turned, b5 * NE + e5)
                        nc.scalar.activation(y_sb[:], y_bank[e5 % 2][:], ACT.Copy).then_inc(y_copied, 1)
                    if out is None and c == 8 and live(b - 1):
                        norm_hi(nc, act, g, n, b - 1, turn_bank)

            each_sequence(act, body)

        @block.vector
        def _(dve):
            def add(b, e):
                dve.wait_ge(y_turned, b * NE + e + 1)
                if e == 0:
                    dve.wait_ge(weight_done, b + 1)
                wait(dve, added, b * NE + e)
                for t in range(QT):
                    rows = g.x_tok[:, tile(b, t), :]
                    last = nc.vector.scalar_tensor_tensor(rows, turn_bank[:, t * P:t * P + P],
                                                          weight[:, t * NE + e:t * NE + e + 1], rows,
                                                          ALU.mult, ALU.add)
                last.then_inc(added, 1)

            def rank_experts(b):
                dve.wait_ge(sc_turned, b + 1)
                nc.vector.tensor_copy(scores[:].rearrange("p (t e) -> p t e", t=QT),
                                      turn_bank[:].rearrange("p (t e) -> p t e", t=QT)[:, :, 0:NE]).then_inc(sc_read, 1)
                dve.wait_ge(sc_read, b + 1)
                other = scores[:].rearrange("p (t j) -> p t j", t=QT).unsqueeze(2).to_broadcast([P, QT, NE, NE])
                this = scores[:].rearrange("p (t e) -> p t e", t=QT).unsqueeze(3).to_broadcast([P, QT, NE, NE])
                by4 = lambda a: a[:].rearrange("p (t e) j -> p t e j", t=QT)
                nc.vector.tensor_tensor(by4(better), other, this, ALU.is_gt).then_inc(compared, 1)
                nc.vector.tensor_tensor(by4(equal), other, this, ALU.is_equal).then_inc(compared, 1)
                dve.wait_ge(compared, b * 5 + 2)
                nc.vector.tensor_tensor(by4(equal), by4(equal),
                                        g.earlier[:].unsqueeze(1).to_broadcast([P, QT, NE, NE]),
                                        ALU.mult).then_inc(compared, 1)
                dve.wait_ge(compared, b * 5 + 3)
                nc.vector.tensor_tensor(better[:], better[:], equal[:], ALU.add).then_inc(compared, 1)
                dve.wait_ge(compared, b * 5 + 4)
                nc.vector.tensor_reduce(rank[:], better[:], AX.X, ALU.add).then_inc(compared, 1)
                dve.wait_ge(compared, b * 5 + 5)
                nc.vector.scalar_tensor_tensor(weight[:], rank[:], 2.0, scores[:], ALU.is_lt,
                                               ALU.mult).then_inc(weight_done, 1)

            def body(b):
                for c in range(EC):
                    m = b * EC + c
                    if live(b):
                        dve.wait_ge(up_full, m + 1)
                        dve.wait_ge(silu_done, m + 1)
                        wait(dve, lo_done, m - 1)
                        nc.vector.tensor_tensor(hidden[c % 2][:], act_gate[c % 2][:], up_bank[c % 2][:],
                                                ALU.mult).then_inc(hidden_done, 1)
                    b1, c1 = lagging(b, c, 1)
                    if live(b1):
                        dve.wait_ge(hi_done, m)
                        hi, lo = hidden_parts[c1 % 3]
                        nc.vector.tensor_tensor(lo[:], hidden[c1 % 2][:], hi[:].bitcast(F32),
                                                ALU.subtract).then_inc(lo_done, 1)
                    if c == 5 and live(b):
                        rank_experts(b)
                    b6, c6 = lagging(b, c, 6)
                    if c6 % NC == 0 and live(b6):
                        add(b6, c6 // NC)
                    if out is None and live(b - 1):
                        if c == 4:
                            wait_apart(nc, dve, g, added, b * NE)
                            norm_stats(nc, dve, g, n, b - 1)
                        if c == 7:
                            norm_apply(nc, dve, g, n, b - 1)
                        if c == 8:
                            norm_lo(nc, dve, g, n, b - 1, turn_bank)

            each_sequence(dve, body)

        @block.gpsimd
        def _(pool):
            if out is None:
                norm_rstd(nc, pool, g, n, 0)
                with pool.Fori(1, NB) as b:
                    norm_rstd(nc, pool, g, n, b)

        @block.sync
        def _(sp):
            if out is not None:
                with sp.Fori(0, NB) as b:
                    sp.wait_ge(added, b * NE + NE)
                    sp.dma_start(out[bass.ds(b * T, T), :].rearrange("(t p) d -> p t d", p=P),
                                 g.x_tok[:, bass.ds(b * QT, QT), :]).then_inc(stored, 16)
                sp.wait_ge(stored, NB * 16)



def attention_b(nc, g):
    VQ = 4
    VW = QT * VQ * 2 * KD
    turn_at, qk_at, v_at, at = [], {}, {}, 0
    for h in range(NH):
        if h % 2 and h < NH - 1:
            qk_at[(h + 1) // 2] = at
            at += 2
        turn_at.append(at)
        at += 3
        if h == 0:
            qk_at[0] = at
            at += 2
        if h % VQ == 0:
            v_at[h // VQ] = at
            at += 2
    RB = at
    assert RB % 3 == 0
    with ExitStack() as ctx:
        hd = Head(nc, ctx, "b", g, 2, 2 * VW)
        sb = lambda n, s, d: ctx.enter_context(nc.sbuf_tensor(n, s, d))
        n = Norm(nc, ctx, "n3", hd.z)
        q = (sb("q_hi", [P, T], F32R), sb("q_lo", [P, T], F32R))
        k = (sb("k_hi", [P, T], F32R), sb("k_lo", [P, T], F32R))
        block = ctx.enter_context(nc.Block())

        def entry(b, at):
            return b * RB - 3 + at

        def v_parts(quarter, i):
            v = hd.v[:, quarter % 2 * VW + i * VW // 2:quarter % 2 * VW + (i + 1) * VW // 2]
            v = v.rearrange("p (h c) -> p h c", c=2 * KD)
            return v[:, :, 0:KD], v[:, :, KD:2 * KD], lambda bank: bank[:].rearrange("p (h c) -> p h c", c=KD)

        def head_at(b, h, lag):
            return (b, h - lag) if h >= lag else (b - 1, h - lag + NH)

        @block.sync
        def _(sp):
            load_x_cur(sp, g, hd, 0)
            with sp.Fori(1, NB) as b:
                sp.wait_ge(hd.filled, entry(b - 1, qk_at[NP - 1] + 2))
                load_x_cur(sp, g, hd, b)

        @block.gpsimd
        def _(pool):
            def body(b):
                for h in range(NH):
                    if live(b):
                        head_probs(nc, pool, hd, b * NH + h, hd.probs[h % 2])
                    if live(b - 1) and h == 3:
                        norm_rstd(nc, pool, g, n, b - 1)

            each_sequence(pool, body)

        @block.tensor
        def _(pe):
            def project(b, p):
                for i, w in enumerate((g.b_q, g.b_k)):
                    r = entry(b, qk_at[p] + i)
                    wait(pe, hd.ring_lo, r - 2)
                    three_passes(nc, hd.ring[(qk_at[p] + i) % 3][:], [v[:, p * P:p * P + P] for v in w],
                                 [x[:] for x in hd.x_cur], True, True).then_inc(hd.filled, 1)

            def values(b, quarter):
                cols = slice(quarter * VQ * KD, (quarter + 1) * VQ * KD)
                for i in range(2):
                    r = entry(b, v_at[quarter] + i)
                    wait(pe, hd.ring_lo, r - 2)
                    for j in range(2):
                        t = 2 * i + j
                        last = three_passes(nc, hd.ring[(v_at[quarter] + i) % 3][:, j * VQ * KD:(j + 1) * VQ * KD],
                                            [x[:, t * P:t * P + P] for x in hd.x_cur],
                                            [v[:, cols] for v in g.b_v], True, True)
                    last.then_inc(hd.filled, 1)

            def scores(b, h):
                if h % 2 == 0:
                    pe.wait_ge(hd.ring_lo, entry(b, qk_at[h // 2] + 2))
                rows = slice(h % 2 * KD, h % 2 * KD + KD)
                for i in range(QT):
                    wait(pe, hd.exp_done, (b * NH + h) * QT + i - 1)
                    keys = (i + 1) * P
                    st = [v[rows, i * P:i * P + P] for v in q]
                    mv = [v[rows, 0:keys] for v in k]
                    three_passes(nc, hd.s_bank[i % 2][:, 0:keys], st, mv, True, False)
                    head_mask(nc, hd, i).then_inc(hd.s_full, 1)

            def body(b):
                for h in range(NH):
                    u = b * NH + h
                    b2, h2 = head_at(b, h, 2)
                    b1, h1 = head_at(b, h, 1)
                    if live(b) and h:
                        scores(b, h)
                    if live(b) and h % 2 and h < NH - 1:
                        project(b, (h + 1) // 2)
                    if live(b2):
                        v0 = h2 // VQ % 2 * VW + h2 % VQ * 2 * KD
                        r_end = entry(b, turn_at[h - 1] + 3) if h else entry(b - 1, turn_at[NH - 1] + 3)
                        head_pv(nc, pe, hd, u - 2, r_end, lambda j: v0 + j * VQ * 2 * KD)
                    if live(b1):
                        head_transpose(nc, pe, hd, u - 1, hd.probs[h1 % 2], entry(b, turn_at[h]), turn_at[h])
                    if live(b) and h == 0:
                        pe.wait_ge(hd.x_cur_in, b * 32 + 32)
                        project(b, 0)
                    if live(b) and h % VQ == 0:
                        values(b, h // VQ)
                    b4, h4 = head_at(b, h, 4)
                    if h4 % 2 == 0 and live(b4):
                        p = h4 // 2
                        pe.wait_ge(hd.y_lo_done, b4 * NP + p + 1)
                        if p == 0:
                            wait(pe, hd.z_done, b4)
                        last = three_passes(nc, hd.z_bank[:], [w[:, p * P:p * P + P] for w in g.b_w],
                                            [y[:] for y in hd.y_parts], p == 0, p == NP - 1)
                        if p == NP - 1:
                            last.then_inc(hd.z_full, 1)
                    if live(b) and h == 0:
                        scores(b, 0)
                    if live(b - 1) and h == 3:
                        output_transpose(nc, pe, hd, b - 1)
                    if live(b - 1) and h == 6:
                        norm_transpose(nc, pe, g, n, b - 1, hd.aux_bank)

            each_sequence(pe, body)

        @block.scalar
        def _(act):
            def project_hi(b, p):
                for i, v in enumerate((q, k)):
                    split_hi(nc, act, hd, entry(b, qk_at[p] + i), qk_at[p] + i, v[0][:])

            def body(b):
                for h in range(NH):
                    u = b * NH + h
                    b3, h3 = head_at(b, h, 3)
                    if live(b) and h:
                        head_exp(nc, act, hd, u, hd.probs[h % 2])
                    if live(b) and h % 2 and h < NH - 1:
                        project_hi(b, (h + 1) // 2)
                    b2, h2 = head_at(b, h, 2)
                    if live(b2):
                        head_low(nc, act, hd, u - 2, h2 % 2 * KD, b2 * NP + h2 // 2)
                    if live(head_at(b, h, 1)[0]):
                        head_transposed_hi(nc, act, hd, entry(b, turn_at[h]), turn_at[h])
                    if live(b) and h == 0:
                        project_hi(b, 0)
                    if live(b) and h % VQ == 0:
                        for i in range(2):
                            hi, lo, bank = v_parts(h // VQ, i)
                            split_hi(nc, act, hd, entry(b, v_at[h // VQ] + i), v_at[h // VQ] + i, hi, bank)
                    if h3 % 2 == 0 and live(b3):
                        act.wait_ge(hd.y_done, u - 1)
                        nc.scalar.activation(hd.y_parts[0][:], hd.y[:], ACT.Copy).then_inc(hd.y_hi_done, 1)
                    if live(b) and h == 0:
                        head_exp(nc, act, hd, u, hd.probs[0])
                    if live(b - 1) and h == 2:
                        output_copy(nc, act, hd, b - 1)
                    if live(b - 1) and h == 6:
                        norm_hi(nc, act, g, n, b - 1, hd.aux_bank)

            each_sequence(act, body)

        @block.vector
        def _(dve):
            def project_lo(b, p):
                for i, v in enumerate((q, k)):
                    split_lo(nc, dve, hd, entry(b, qk_at[p] + i), qk_at[p] + i, v[1][:], v[0][:])

            def body(b):
                for h in range(NH):
                    u = b * NH + h
                    b3, h3 = head_at(b, h, 3)
                    b2, h2 = head_at(b, h, 2)
                    if live(b) and h:
                        head_max(nc, dve, hd, u)
                    if live(b) and h % 2 and h < NH - 1:
                        project_lo(b, (h + 1) // 2)
                    if live(b2):
                        head_y(nc, dve, hd, u - 2, h2 % 2 * KD)
                    if live(b) and h:
                        head_recip(nc, dve, hd, u)
                    if live(head_at(b, h, 1)[0]):
                        head_transposed_lo(nc, dve, hd, entry(b, turn_at[h]), turn_at[h])
                    if live(b) and h == 0:
                        project_lo(b, 0)
                    if live(b) and h % VQ == 0:
                        for i in range(2):
                            hi, lo, bank = v_parts(h // VQ, i)
                            split_lo(nc, dve, hd, entry(b, v_at[h // VQ] + i), v_at[h // VQ] + i, lo, hi, bank)
                    if h3 % 2 == 0 and live(b3):
                        dve.wait_ge(hd.y_hi_done, b3 * NP + h3 // 2 + 1)
                        nc.vector.tensor_tensor(hd.y_parts[1][:], hd.y[:], hd.y_parts[0][:].bitcast(F32),
                                                ALU.subtract).then_inc(hd.y_lo_done, 1)
                    if live(b) and h == 0:
                        head_max(nc, dve, hd, u)
                        head_recip(nc, dve, hd, u)
                    if live(b - 1) and h == 3:
                        output_add(nc, dve, g, hd, b - 1)
                        norm_stats(nc, dve, g, n, b - 1)
                    if live(b - 1) and h == 5:
                        norm_apply(nc, dve, g, n, b - 1)
                    if live(b - 1) and h == 6:
                        norm_lo(nc, dve, g, n, b - 1, hd.aux_bank)

            each_sequence(dve, body)



def build(nc, ins, out):
    g = Shared()
    with ExitStack() as ctx:
        sb = lambda n, s, d: ctx.enter_context(nc.sbuf_tensor(n, s, d))
        pair = lambda n, s: (sb(f"{n}_hi", s, F32R), sb(f"{n}_lo", s, F32R))
        g.x_tok = sb("x_tok", [P, NB * QT, D], F32)
        g.xn_hi, g.xn_lo = pair("xn", [P, NB * T])
        g.w1, g.w2 = pair("w1", [P, EHP]), pair("w2", [P, EHP])
        g.w3 = pair("w3", [P, EC * P])
        g.wg = pair("wg", [P, P])
        g.b_q, g.b_k, g.b_v = (pair(f"b_{c}", [P, NH * KD]) for c in "qkv")
        g.b_w = pair("b_w", [P, NP * P])
        g.ident = sb("ident", [P, P], F32)
        g.ident_bf = sb("ident_bf", [P, P], BF16)
        g.mask = sb("mask", [P, P], BF16)
        g.earlier = sb("earlier", [P, NE, NE], F32)
        g.minus_half = sb("minus_half", [P, QT], F32)
        g.eps = sb("eps", [P, QT], F32)
        g.unused = sb("unused", [P, 1], F32)
        with ExitStack() as first:
            sb1 = lambda n, s: first.enter_context(nc.sbuf_tensor(n, s, F32R))
            pair1 = lambda n, s: (sb1(f"{n}_hi", s), sb1(f"{n}_lo", s))
            g.a_wq, g.a_wk = pair1("a_wq", [P, P]), pair1("a_wk", [P, P])
            g.a_wv1, g.a_wv2 = pair1("a_wv1", [P, KD]), pair1("a_wv2", [KD, D])
            prepare(nc, g, ins)
            attention_a(nc, g)
        experts(nc, g, "f1")
        attention_b(nc, g)
        experts(nc, g, "f2", out)


_INS = ['L0_attn_a_x', 'L0_attn_a_w_q', 'L0_attn_a_w_k', 'L0_attn_a_w_v1', 'L0_attn_a_w_v2', 'L0_attn_b_Q',
        'L0_attn_b_K', 'L0_attn_b_V', 'L0_attn_b_W', 'L0_ffn_Wg', 'L0_ffn_W1', 'L0_ffn_W2', 'L0_ffn_W3']


def kernel(**inputs):
    import numpy as _np
    import concourse.bacc as _bacc
    from concourse import mybir as _mybir
    from concourse.bass_utils import run_bass_kernel_spmd as _run

    nc = _bacc.Bacc("TRN2", target_bir_lowering=False, num_devices=1)
    arrays, args = {}, []
    for name in _INS:
        a = _np.ascontiguousarray(inputs[name])
        arrays[f"in_{name}_dram"] = a
        args.append(nc.dram_tensor(f"in_{name}_dram", a.shape, _mybir.dt.from_np(a.dtype), kind="ExternalInput").ap())
    out = nc.dram_tensor("out_0_dram", (NB * T, D), _mybir.dt.float32, kind="ExternalOutput").ap()
    build(nc, args, out)
    r = _run(nc, [arrays], core_ids=[0])
    return _np.asarray(r.results[0]["out_0_dram"]).reshape(NB, T, D)
```

```python
import concourse.bass as bass
from concourse import mybir
from contextlib import ExitStack

F32 = mybir.dt.float32
F32R = mybir.dt.float32r
BF16 = mybir.dt.bfloat16
ALU = mybir.AluOpType
ACT = mybir.ActivationFunctionType
AX = mybir.AxisListType

P = 128
NB, T, D = 8, 512, 128
QT = T // P
KD = 64
NH = 16
NP = NH // 2
NE, EH = 8, 352
NC = 3
EC = NE * NC
LAST = EH - 2 * P
EHP = 2848
EPS = 1e-5
MASKED = -3.0e38

P_AT = [0, 128, 384, 768]
PT_AT = {0: 0, 1: 512, 3: 896, 2: 1024}
PT_BANKS = [((0,), 0, 512), ((1, 3), 512, 512), ((2,), 1024, 256)]
NPT = 1280
S_GROUPS = ((0, 1), (2,), (3,))
S_AT = {0: (0, 0), 1: (0, P), 2: (1, 0), 3: (2, 0)}


def live(b):
    return not isinstance(b, int) or 0 <= b < NB


def wait(eng, sem, value):
    if not isinstance(value, int) or value > 0:
        eng.wait_ge(sem, value)


def wait_apart(nc, dve, g, sem, value):
    wait(dve, sem, value)
    if not isinstance(value, int):
        nc.vector.memset(g.unused[:], 0.0)


def tokens(b):
    return bass.ds(b * T, T)


def tile(b, t):
    return b * QT + t


def three_passes(nc, out, st, mv, start, stop):
    nc.tensor.matmul(out, st[0], mv[0], start=start, stop=False)
    nc.tensor.matmul(out, st[0], mv[1], start=False, stop=False)
    return nc.tensor.matmul(out, st[1], mv[0], start=False, stop=stop)


class Shared:
    pass


def each_sequence(eng, body):
    body(0)
    body(1)
    with eng.Fori(2, NB) as b:
        body(b)
    body(NB)



class Norm:

    def __init__(self, nc, ctx, name, xn=None):
        sb = lambda n, s, d: ctx.enter_context(nc.sbuf_tensor(f"{name}_{n}", s, d))
        sem = lambda n: ctx.enter_context(nc.semaphore(f"{name}_{n}"))
        self.stats = sb("stats", [P, QT, 6], F32)
        self.mv = sb("mv", [P, QT, 2], F32)
        self.veps = sb("veps", [P, QT], F32)
        self.rstd = sb("rstd", [P, QT], F32)
        self.xn = sb("xn", [P, T], F32) if xn is None else xn
        self.stats_done = sem("stats_done")
        self.mv_done = sem("mv_done")
        self.veps_done = sem("veps_done")
        self.rstd_done = sem("rstd_done")
        self.xn_done = sem("xn_done")
        self.xnt_full = sem("xnt_full")
        self.hi_done = sem("hi_done")
        self.lo_done = sem("lo_done")


def norm_stats(nc, dve, g, n, b):
    for t in range(QT):
        nc.vector.bn_stats(n.stats[:, t, :], g.x_tok[:, tile(b, t), :]).then_inc(n.stats_done, 1)
    wait(dve, n.rstd_done, b)
    wait_apart(nc, dve, g, n.stats_done, b * QT + QT)
    for t in range(QT):
        nc.vector.bn_aggr(n.mv[:, t, :], n.stats[:, t, :]).then_inc(n.mv_done, 1)


def norm_rstd(nc, pool, g, n, b):
    wait(pool, n.xn_done, b * QT)
    pool.wait_ge(n.mv_done, b * QT + QT)
    nc.gpsimd.tensor_tensor(n.veps[:], n.mv[:, :, 1], g.eps[:], ALU.add).then_inc(n.veps_done, 1)
    pool.wait_ge(n.veps_done, b + 1)
    nc.gpsimd.tensor_tensor(n.rstd[:], n.veps[:], g.minus_half[:], ALU.pow).then_inc(n.rstd_done, 1)


def norm_apply(nc, dve, g, n, b, xn_free=False):
    dve.wait_ge(n.rstd_done, b + 1)
    dve.wait_ge(n.mv_done, b * QT + QT)
    if not xn_free:
        wait(dve, n.xnt_full, b)
    for t in range(QT):
        nc.vector.tensor_scalar(n.xn[:, t * D:t * D + D], g.x_tok[:, tile(b, t), :], n.mv[:, t, 0:1], n.rstd[:, t:t + 1],
                                ALU.subtract, ALU.mult).then_inc(n.xn_done, 1)


def norm_transpose(nc, pe, g, n, b, bank):
    pe.wait_ge(n.xn_done, b * QT + QT)
    for t in range(QT):
        last = nc.tensor.transpose(bank[:, t * P:t * P + P], n.xn[:, t * D:t * D + D], g.ident[:])
    last.then_inc(n.xnt_full, 1)


def norm_hi(nc, act, g, n, b, bank):
    act.wait_ge(n.xnt_full, b + 1)
    nc.scalar.activation(g.xn_hi[:, tokens(b)], bank[:], ACT.Copy).then_inc(n.hi_done, 1)


def norm_lo(nc, dve, g, n, b, bank):
    dve.wait_ge(n.hi_done, b + 1)
    nc.vector.tensor_tensor(g.xn_lo[:, tokens(b)], bank[:], g.xn_hi[:, tokens(b)].bitcast(F32),
                            ALU.subtract).then_inc(n.lo_done, 1)



def prepare(nc, g, ins):
    x, w_q, w_k, w_v1, w_v2, Q, K, V, W, Wg, W1, W2, W3 = ins
    with ExitStack() as ctx:
        sb = lambda n, s, d: ctx.enter_context(nc.sbuf_tensor(n, s, d))
        pb = lambda n: ctx.enter_context(nc.psum_tensor(n, [P, 512], F32))
        sem = lambda n: ctx.enter_context(nc.semaphore(n))
        n = Norm(nc, ctx, "n0")
        a_raw = sb("a_raw", [P, 3, P], F32)
        v2_raw = sb("v2_raw", [KD, P], F32)
        wg_raw = sb("wg_raw", [NE, D], F32)
        f_raw = [sb(f"f_raw{i}", [P, EHP], F32) for i in range(2)]
        w3_raw = f_raw[0]
        qkv_raw = [sb(f"qkv_raw{i}", [P, KD, NH], F32) for i in range(4)]
        w_perm = sb("w_perm", [P, NH * KD], F32)
        norm_bank = [pb(f"norm_bank{i}") for i in range(2)]
        bank = [pb(f"prep_bank{i}") for i in range(4)]
        x_in = [sem(f"x_in{b}") for b in range(NB)]
        a_in = sem("a_in")
        wg_in = sem("wg_in")
        f_in = [sem(f"f_in{i}") for i in range(3)]
        b_in = [sem(f"b_in{i}") for i in range(4)]
        zeroed = sem("zeroed")
        consts = sem("consts")
        direct_hi = sem("direct_hi")
        direct_lo = sem("direct_lo")
        perm_done = sem("perm_done")
        turned = sem("turned")
        turned_hi = sem("turned_hi")
        turned_lo = sem("turned_lo")

        direct = [
            (a_raw[:, 0, :], KD ** -0.5, g.a_wq[0][:], g.a_wq[1][:], a_in, 96),
            (a_raw[:, 1, :], 1.0, g.a_wk[0][:], g.a_wk[1][:], a_in, 96),
            (a_raw[:, 2, 0:KD], 1.0, g.a_wv1[0][:], g.a_wv1[1][:], a_in, 96),
            (v2_raw[:], 1.0, g.a_wv2[0][:], g.a_wv2[1][:], a_in, 96),
        ]
        for i, (parts, scale) in enumerate(((g.b_q, 1.0 / 128), (g.b_k, 1.0), (g.b_v, 1.0))):
            raw = qkv_raw[i][:].rearrange("p q h -> p h q")
            hi, lo = (part[:].rearrange("p (h q) -> p h q", h=NH) for part in parts)
            direct.append((raw, scale, hi, lo, b_in[i], 16))

        groups = [([(wg_raw[:], g.ident[0:NE, 0:NE], NE)], wg_in, 16,
                   g.wg[0][:, 0:NE], g.wg[1][:, 0:NE])]
        for i, parts in enumerate((g.w1, g.w2)):
            for j in range(0, 22, 4):
                m = min(4, 22 - j)
                groups.append(([(f_raw[i][:, (j + k) * P:(j + k) * P + P], g.ident[:], P) for k in range(m)], f_in[i], 16,
                               parts[0][:, j * P:(j + m) * P], parts[1][:, j * P:(j + m) * P]))
        for c in range(0, EC, 4):
            at = [(c + k) // NC * EH + (c + k) % NC * P for k in range(4)]
            groups.append(([(w3_raw[:, a:a + P], g.ident[:], P) for a in at], f_in[2], 16,
                           g.w3[0][:, c * P:(c + 4) * P], g.w3[1][:, c * P:(c + 4) * P]))
        for p in range(0, NP, 4):
            groups.append(([(w_perm[:, (p + k) * P:(p + k) * P + P], g.ident[:], P) for k in range(4)],
                           perm_done, 1, g.b_w[0][:, p * P:(p + 4) * P], g.b_w[1][:, p * P:(p + 4) * P]))

        block = ctx.enter_context(nc.Block())

        @block.sync
        def _(sp):
            for b in range(NB):
                sp.dma_start(g.x_tok[:, b * QT:b * QT + QT, :],
                             x[b].rearrange("(t p) d -> p t d", p=P)).then_inc(x_in[b], 16)
                if b == 0:
                    for k in range(2):
                        sp.dma_start(a_raw[:, 0, k * KD:k * KD + KD], w_q).then_inc(a_in, 16)
                        sp.dma_start(a_raw[:, 1, k * KD:k * KD + KD], w_k).then_inc(a_in, 16)
                    sp.dma_start(a_raw[:, 2, 0:KD], w_v1).then_inc(a_in, 16)
                    sp.dma_start(v2_raw[:], w_v2).then_inc(a_in, 16)
            sp.dma_start(wg_raw[:], Wg).then_inc(wg_in, 16)
            for i, w in enumerate((W1, W2)):
                flat = w.rearrange("e h d -> (e h) d").rearrange("(j p) d -> p j d", p=P)
                sp.dma_start(f_raw[i][:, 0:NE * EH].rearrange("p (j d) -> p j d", d=D), flat).then_inc(f_in[i], 16)
            for i, w in enumerate((Q, K, V)):
                sp.dma_start(qkv_raw[i][:], w.rearrange("q d h -> d q h")).then_inc(b_in[i], 16)
            sp.dma_start(qkv_raw[3][:], W).then_inc(b_in[3], 16)
            sp.wait_ge(turned, 7)
            sp.dma_start(w3_raw[:, 0:NE * EH].rearrange("p (e h) -> p e h", e=NE),
                         W3.rearrange("e d h -> d e h")).then_inc(f_in[2], 16)

        @block.gpsimd
        def _(pool):
            nc.gpsimd.memset(g.ident[:], 0.0).then_inc(zeroed, 1)
            nc.gpsimd.memset(g.ident_bf[:], 0.0).then_inc(zeroed, 1)
            nc.gpsimd.memset(g.mask[:], 0.0).then_inc(zeroed, 1)
            nc.gpsimd.memset(g.earlier[:], 0.0).then_inc(zeroed, 1)
            nc.gpsimd.memset(g.minus_half[:], -0.5).then_inc(consts, 1)
            nc.gpsimd.memset(g.eps[:], EPS).then_inc(consts, 1)
            for part in g.wg:
                nc.gpsimd.memset(part[:].bitcast(F32), 0.0).then_inc(consts, 1)
            nc.gpsimd.memset(w3_raw[:, NE * EH:EHP], 0.0).then_inc(consts, 1)
            for part in g.w1 + g.w2:
                nc.gpsimd.memset(part[:, NE * EH:EHP].bitcast(F32), 0.0).then_inc(consts, 1)
            pool.wait_ge(zeroed, 4)
            for idn in (g.ident, g.ident_bf):
                nc.gpsimd.affine_select(out=idn[:], in_=idn[:], compare_op=ALU.not_equal, fill=1.0, base=0,
                                        pattern=[[-1, P]], channel_multiplier=1).then_inc(consts, 1)
            nc.gpsimd.affine_select(out=g.mask[:], in_=g.mask[:], compare_op=ALU.is_ge, fill=MASKED, base=0,
                                    pattern=[[-1, P]], channel_multiplier=1).then_inc(consts, 1)
            nc.gpsimd.affine_select(out=g.earlier[:], in_=g.earlier[:], compare_op=ALU.is_ge, fill=1.0, base=0,
                                    pattern=[[-1, NE], [1, NE]], channel_multiplier=0).then_inc(consts, 1)
            pool.wait_ge(consts, 13)
            norm_rstd(nc, pool, g, n, 0)
            with pool.Fori(1, NB) as b:
                norm_rstd(nc, pool, g, n, b)

        @block.vector
        def _(dve):
            dve.wait_ge(consts, 13)
            for i in range(4):
                raw, scale, hi, lo, loaded, count = direct[i]
                dve.wait_ge(direct_hi, i + 1)
                nc.vector.scalar_tensor_tensor(lo, raw, scale, hi.bitcast(F32), ALU.mult,
                                               ALU.subtract).then_inc(direct_lo, 1)
            for b in range(NB):
                dve.wait_ge(x_in[b], 16)
            norm_stats(nc, dve, g, n, 0)
            norm_apply(nc, dve, g, n, 0)
            with dve.Fori(1, NB) as b:
                norm_stats(nc, dve, g, n, b)
                norm_lo(nc, dve, g, n, b - 1, norm_bank[0])
                norm_apply(nc, dve, g, n, b)
            norm_lo(nc, dve, g, n, NB - 1, norm_bank[0])
            dve.wait_ge(b_in[3], 16)
            nc.vector.tensor_scalar(w_perm[:].rearrange("p (h v) -> p h v", h=NH), qkv_raw[3][:].rearrange("p v h -> p h v"), 1.0 / NH, None,
                                    ALU.mult).then_inc(perm_done, 1)
            for i in range(4, len(direct)):
                raw, scale, hi, lo, loaded, count = direct[i]
                dve.wait_ge(direct_hi, i + 1)
                nc.vector.scalar_tensor_tensor(lo, raw, scale, hi.bitcast(F32), ALU.mult,
                                               ALU.subtract).then_inc(direct_lo, 1)
            for i, (tiles, loaded, count, hi, lo) in enumerate(groups):
                dve.wait_ge(turned_hi, i + 1)
                nc.vector.tensor_tensor(lo, bank[i % 4][:, 0:len(tiles) * tiles[0][2]], hi.bitcast(F32),
                                        ALU.subtract).then_inc(turned_lo, 1)

        @block.scalar
        def _(act):
            act.wait_ge(consts, 13)
            for i in range(4):
                raw, scale, hi, lo, loaded, count = direct[i]
                act.wait_ge(loaded, count)
                nc.scalar.activation(hi, raw, ACT.Copy, scale=scale).then_inc(direct_hi, 1)
            with act.Fori(0, NB) as b:
                norm_hi(nc, act, g, n, b, norm_bank[0])
            for i in range(4, len(direct)):
                raw, scale, hi, lo, loaded, count = direct[i]
                act.wait_ge(loaded, count)
                nc.scalar.activation(hi, raw, ACT.Copy, scale=scale).then_inc(direct_hi, 1)
            for i, (tiles, loaded, count, hi, lo) in enumerate(groups):
                act.wait_ge(turned, i + 1)
                nc.scalar.activation(hi, bank[i % 4][:, 0:len(tiles) * tiles[0][2]], ACT.Copy).then_inc(turned_hi, 1)

        @block.tensor
        def _(pe):
            pe.wait_ge(consts, 13)
            norm_transpose(nc, pe, g, n, 0, norm_bank[0])
            with pe.Fori(1, NB) as b:
                pe.wait_ge(n.lo_done, b)
                norm_transpose(nc, pe, g, n, b, norm_bank[0])
            for i, (tiles, loaded, count, hi, lo) in enumerate(groups):
                pe.wait_ge(loaded, count)
                wait(pe, turned_lo, i - 3)
                for k, (src, ident, width) in enumerate(tiles):
                    last = nc.tensor.transpose(bank[i % 4][:, k * width:k * width + width], src, ident)
                last.then_inc(turned, 1)



class Head:

    def __init__(self, nc, ctx, name, g, probs, v_cols):
        sb = lambda n, s, d: ctx.enter_context(nc.sbuf_tensor(f"{name}_{n}", s, d))
        pb = lambda n: ctx.enter_context(nc.psum_tensor(f"{name}_{n}", [P, 512], F32))
        sem = lambda n: ctx.enter_context(nc.semaphore(f"{name}_{n}"))
        self.ident, self.ident_bf, self.mask = g.ident, g.ident_bf, g.mask
        self.probs = [sb(f"probs{i}", [P, NPT], F32) for i in range(probs)]
        self.pt = (sb("pt_hi", [P, NPT], F32R), sb("pt_lo", [P, NPT], F32R))
        self.neg_max = sb("neg_max", [P, QT], F32)
        self.sums = sb("sums", [P, QT], F32)
        self.recip = sb("recip", [P, QT], F32)
        self.v = sb("v", [P, v_cols], F32R)
        self.y = sb("y", [P, T], F32)
        self.y_parts = (sb("y_hi", [P, T], F32R), sb("y_lo", [P, T], F32R))
        self.z = sb("z", [P, T], F32)
        self.x_cur = (sb("x_cur_hi", [P, T], F32R), sb("x_cur_lo", [P, T], F32R))
        self.s_bank = [pb(f"s_bank{i}") for i in range(len(S_GROUPS))]
        self.ring = [pb(f"ring{i}") for i in range(3)]
        self.pv_bank = pb("pv_bank")
        self.z_bank = pb("z_bank")
        self.filled = sem("filled")
        self.ring_hi = sem("ring_hi")
        self.ring_lo = sem("ring_lo")
        self.s_full = sem("s_full")
        self.max_done = sem("max_done")
        self.exp_done = sem("exp_done")
        self.recip_done = sem("recip_done")
        self.probs_done = sem("probs_done")
        self.pv_full = sem("pv_full")
        self.low_done = sem("low_done")
        self.y_done = sem("y_done")
        self.y_hi_done = sem("y_hi_done")
        self.y_lo_done = sem("y_lo_done")
        self.z_full = sem("z_full")
        self.z_done = sem("z_done")
        self.zt_full = sem("zt_full")
        self.x_done = sem("x_done")
        self.x_cur_in = sem("x_cur_in")


def split_hi(nc, act, hd, r, n, dst, src=lambda bank: bank[:]):
    act.wait_ge(hd.filled, r + 1)
    nc.scalar.activation(dst, src(hd.ring[n % 3]), ACT.Copy).then_inc(hd.ring_hi, 1)


def split_lo(nc, dve, hd, r, n, dst, hi, src=lambda bank: bank[:]):
    dve.wait_ge(hd.ring_hi, r + 1)
    nc.vector.tensor_tensor(dst, src(hd.ring[n % 3]), hi.bitcast(F32), ALU.subtract).then_inc(hd.ring_lo, 1)


def head_transpose(nc, pe, hd, u, probs, k, n):
    if k == 0:
        pe.wait_ge(hd.probs_done, u * QT + QT)
    key_tiles, at, width = PT_BANKS[k]
    for j in key_tiles:
        for i in range(j, QT):
            to = PT_AT[j] - at + (i - j) * P
            last = nc.tensor.transpose(hd.ring[n % 3][:, to:to + P],
                                       probs[:, P_AT[i] + j * P:P_AT[i] + j * P + P], hd.ident[:])
    last.then_inc(hd.filled, 1)


def head_transposed_hi(nc, act, hd, r, n, k):
    _, at, width = PT_BANKS[k]
    split_hi(nc, act, hd, r, n, hd.pt[0][:, at:at + width], lambda bank: bank[:, 0:width])


def head_transposed_lo(nc, dve, hd, r, n, k):
    _, at, width = PT_BANKS[k]
    split_lo(nc, dve, hd, r, n, hd.pt[1][:, at:at + width], hd.pt[0][:, at:at + width],
             lambda bank: bank[:, 0:width])


def s_tile(hd, i, at=0):
    bank, col = S_AT[i]
    return hd.s_bank[bank][:, col + at:col + (i + 1) * P]


def s_free(pe, hd, u, group):
    wait(pe, hd.exp_done, (u - 1) * QT + S_GROUPS[group][-1] + 1)


def head_mask(nc, hd, i):
    return nc.tensor.matmul(s_tile(hd, i, i * P), hd.ident_bf[:], hd.mask[:], start=False, stop=True)


def head_max(nc, dve, hd, u, group):
    dve.wait_ge(hd.s_full, u * len(S_GROUPS) + group + 1)
    for i in S_GROUPS[group]:
        nc.vector.tensor_reduce(hd.neg_max[:, i:i + 1], s_tile(hd, i), AX.X, ALU.max,
                                negate=True).then_inc(hd.max_done, 1)


def head_exp(nc, act, hd, u, group, probs):
    if group == 0:
        wait(act, hd.recip_done, u)
    act.wait_ge(hd.max_done, u * QT + S_GROUPS[group][-1] + 1)
    for i in S_GROUPS[group]:
        nc.scalar.activation(probs[:, P_AT[i]:P_AT[i] + (i + 1) * P], s_tile(hd, i),
                             ACT.Exp, bias=hd.neg_max[:, i:i + 1],
                             accum_out=hd.sums[:, i:i + 1]).then_inc(hd.exp_done, 1)


def head_recip(nc, dve, hd, u):
    dve.wait_ge(hd.exp_done, u * QT + QT)
    wait(dve, hd.probs_done, u * QT)
    nc.vector.reciprocal(hd.recip[:], hd.sums[:]).then_inc(hd.recip_done, 1)


def head_probs(nc, pool, hd, u, probs):
    pool.wait_ge(hd.recip_done, u + 1)
    for i in range(QT):
        part = probs[:, P_AT[i]:P_AT[i] + (i + 1) * P]
        nc.gpsimd.tensor_tensor(part, part, hd.recip[:, i:i + 1].to_broadcast([P, (i + 1) * P]),
                                ALU.mult).then_inc(hd.probs_done, 1)


def head_pv(nc, pe, hd, u, r_end, v_at):
    pe.wait_ge(hd.ring_lo, r_end)
    wait(pe, hd.y_done, u)
    for j in range(QT):
        v = hd.v[:, v_at(j):v_at(j) + 2 * KD]
        for part in range(2):
            last = nc.tensor.matmul(hd.pv_bank[:, j * P:T], v, hd.pt[part][:, PT_AT[j]:PT_AT[j] + T - j * P],
                                    start=(j == 0 and part == 0), stop=(j == QT - 1 and part == 1))
    last.then_inc(hd.pv_full, 1)


def head_low(nc, act, hd, u, row, split):
    act.wait_ge(hd.pv_full, u + 1)
    wait(act, hd.y_lo_done, split)
    nc.scalar.activation(hd.y[row:row + KD, :], hd.pv_bank[KD:P, :], ACT.Copy).then_inc(hd.low_done, 1)


def head_y(nc, dve, hd, u, row):
    dve.wait_ge(hd.low_done, u + 1)
    y = hd.y[row:row + KD, :]
    nc.vector.tensor_tensor(y, hd.pv_bank[0:KD, :], y, ALU.add).then_inc(hd.y_done, 1)


def output_copy(nc, act, hd, full):
    act.wait_ge(hd.z_full, full)
    nc.scalar.activation(hd.z[:], hd.z_bank[:], ACT.Copy).then_inc(hd.z_done, 1)


def output_transpose(nc, pe, hd, b):
    pe.wait_ge(hd.z_done, b + 1)
    for t in range(QT):
        last = nc.tensor.transpose(hd.z_bank[:, t * P:t * P + P], hd.z[:, t * P:t * P + P], hd.ident[:])
    last.then_inc(hd.zt_full, 1)


def output_add(nc, dve, g, hd, b):
    dve.wait_ge(hd.zt_full, b + 1)
    rows = g.x_tok[:, bass.ds(b * QT, QT), :]
    nc.vector.tensor_tensor(rows, rows, hd.z_bank[:].rearrange("p (t d) -> p t d", t=QT),
                            ALU.add).then_inc(hd.x_done, 1)
    wait_apart(nc, dve, g, hd.x_done, b + 1)


def load_x_cur(sp, g, hd, b):
    for part, src in zip(hd.x_cur, (g.xn_hi, g.xn_lo)):
        sp.dma_start(part[:].bitcast(F32), src[:, tokens(b)].bitcast(F32)).then_inc(hd.x_cur_in, 16)



def attention_a(nc, g):
    RA = 6
    with ExitStack() as ctx:
        hd = Head(nc, ctx, "a", g, 1, QT * 2 * KD)
        sb = lambda n, s, d: ctx.enter_context(nc.sbuf_tensor(n, s, d))
        n = Norm(nc, ctx, "n1", hd.z)
        q_stack = sb("q_stack", [P, T], F32R)
        k_twice = (sb("k_twice_hi", [P, T], F32R), sb("k_twice_lo", [P, T], F32R))
        v_parts = [hd.v[:].rearrange("p (t v) -> p t v", t=QT)[:, :, k * KD:k * KD + KD] for k in range(2)]
        v_bank = lambda bank: bank[:, 0:QT * KD].rearrange("p (t v) -> p t v", t=QT)
        block = ctx.enter_context(nc.Block())

        def steps(eng, body):
            for b in range(4):
                body(b)
            with eng.Fori(4, NB) as b:
                body(b)
            for b in range(NB, NB + 4):
                body(b)

        def t_at(b):
            return b * RA + 2

        @block.sync
        def _(sp):
            load_x_cur(sp, g, hd, 0)
            with sp.Fori(1, NB) as b:
                sp.wait_ge(hd.filled, t_at(b - 1) + 4)
                load_x_cur(sp, g, hd, b)

        @block.gpsimd
        def _(pool):
            def body(b):
                if live(b):
                    head_probs(nc, pool, hd, b, hd.probs[0])
                if live(b - 3):
                    norm_rstd(nc, pool, g, n, b - 3)

            steps(pool, body)

        @block.tensor
        def _(pe):
            def body(b):
                if live(b - 4):
                    norm_transpose(nc, pe, g, n, b - 4, hd.z_bank)
                if live(b - 2):
                    head_pv(nc, pe, hd, b - 2, t_at(b - 2) + 4, lambda j: j * 2 * KD)
                if live(b - 1):
                    r = t_at(b - 1)
                    for k in range(3):
                        wait(pe, hd.ring_lo, r + k - 2)
                        head_transpose(nc, pe, hd, b - 1, hd.probs[0], k, 2 + k)
                    pe.wait_ge(hd.ring_lo, r + 1)
                    pe.wait_ge(hd.x_cur_in, b * 32)
                    for t in range(QT):
                        last = three_passes(nc, hd.ring[2][:, t * KD:t * KD + KD],
                                            [x[:, t * P:t * P + P] for x in hd.x_cur],
                                            [g.a_wv1[0][:], g.a_wv1[1][:]], True, True)
                    last.then_inc(hd.filled, 1)
                if live(b):
                    for k, w in enumerate((g.a_wq, g.a_wk)):
                        wait(pe, hd.ring_lo, b * RA + k - 2)
                        three_passes(nc, hd.ring[k][:], [w[0][:], w[1][:]],
                                     [x[:, tokens(b)] for x in (g.xn_hi, g.xn_lo)], True,
                                     True).then_inc(hd.filled, 1)
                if live(b - 3):
                    pe.wait_ge(hd.y_lo_done, b - 2)
                    wait(pe, n.lo_done, b - 3)
                    three_passes(nc, hd.z_bank[:], [w[:] for w in g.a_wv2], [y[0:KD, :] for y in hd.y_parts],
                                 True, True).then_inc(hd.z_full, 1)
                if live(b):
                    pe.wait_ge(hd.ring_lo, b * RA + 2)
                    for group, tiles in enumerate(S_GROUPS):
                        s_free(pe, hd, b, group)
                        for i in tiles:
                            for part in range(2):
                                nc.tensor.matmul(s_tile(hd, i), q_stack[:, i * P:i * P + P],
                                                 k_twice[part][:, 0:(i + 1) * P], start=(part == 0), stop=False)
                            last = head_mask(nc, hd, i)
                        last.then_inc(hd.s_full, 1)
                if live(b - 3):
                    output_transpose(nc, pe, hd, b - 3)

            steps(pe, body)

        @block.scalar
        def _(act):
            def body(b):
                if live(b - 4):
                    norm_hi(nc, act, g, n, b - 4, hd.z_bank)
                if live(b - 2):
                    head_low(nc, act, hd, b - 2, 0, b - 2)
                if live(b - 1):
                    for k in range(3):
                        head_transposed_hi(nc, act, hd, t_at(b - 1) + k, 2 + k, k)
                    split_hi(nc, act, hd, t_at(b - 1) + 3, 2, v_parts[0], v_bank)
                if live(b):
                    split_hi(nc, act, hd, b * RA, 0, q_stack[:])
                    split_hi(nc, act, hd, b * RA + 1, 1, k_twice[0][:])
                if live(b - 3):
                    output_copy(nc, act, hd, b - 2)
                if live(b - 2):
                    act.wait_ge(hd.y_done, b - 1)
                    nc.scalar.activation(hd.y_parts[0][0:KD, :], hd.y[0:KD, :], ACT.Copy).then_inc(hd.y_hi_done, 1)
                if live(b):
                    for group in range(len(S_GROUPS)):
                        head_exp(nc, act, hd, b, group, hd.probs[0])

            steps(act, body)

        @block.vector
        def _(dve):
            def body(b):
                if live(b - 4):
                    norm_lo(nc, dve, g, n, b - 4, hd.z_bank)
                if live(b - 2):
                    head_y(nc, dve, hd, b - 2, 0)
                if live(b - 1):
                    for k in range(3):
                        head_transposed_lo(nc, dve, hd, t_at(b - 1) + k, 2 + k, k)
                    split_lo(nc, dve, hd, t_at(b - 1) + 3, 2, v_parts[1], v_parts[0], v_bank)
                if live(b):
                    dve.wait_ge(hd.ring_hi, b * RA + 1)
                    nc.vector.tensor_tensor(q_stack[KD:P, :], hd.ring[0][KD:P, :], q_stack[KD:P, :].bitcast(F32),
                                            ALU.subtract).then_inc(hd.ring_lo, 1)
                    split_lo(nc, dve, hd, b * RA + 1, 1, k_twice[1][:], k_twice[0][:])
                if live(b - 2):
                    dve.wait_ge(hd.y_hi_done, b - 1)
                    nc.vector.tensor_tensor(hd.y_parts[1][0:KD, :], hd.y[0:KD, :], hd.y_parts[0][0:KD, :].bitcast(F32),
                                            ALU.subtract).then_inc(hd.y_lo_done, 1)
                if live(b):
                    for group in range(len(S_GROUPS)):
                        head_max(nc, dve, hd, b, group)
                    head_recip(nc, dve, hd, b)
                if live(b - 3):
                    output_add(nc, dve, g, hd, b - 3)
                    norm_stats(nc, dve, g, n, b - 3)
                    norm_apply(nc, dve, g, n, b - 3)

            steps(dve, body)



def experts(nc, g, name, out=None):
    with ExitStack() as ctx:
        sb = lambda n, s, d: ctx.enter_context(nc.sbuf_tensor(f"{name}_{n}", s, d))
        pb = lambda n: ctx.enter_context(nc.psum_tensor(f"{name}_{n}", [P, 512], F32))
        sem = lambda n: ctx.enter_context(nc.semaphore(f"{name}_{n}"))
        n = Norm(nc, ctx, f"{name}_n")
        act_gate = [sb(f"act_gate{i}", [P, T], F32) for i in range(2)]
        hidden = [sb(f"hidden{i}", [P, T], F32) for i in range(2)]
        hidden_parts = [(sb(f"hidden_hi{i}", [P, T], F32R), sb(f"hidden_lo{i}", [P, T], F32R)) for i in range(3)]
        y_sb = sb("y_sb", [P, T], F32)
        scores_t = sb("scores_t", [P, T], F32)
        scores = sb("scores", [P, QT * NE], F32)
        better = sb("better", [P, QT * NE, NE], F32)
        equal = sb("equal", [P, QT * NE, NE], F32)
        rank = sb("rank", [P, QT * NE], F32)
        weight = sb("weight", [P, QT * NE], F32)
        gate_bank = [pb(f"gate_bank{i}") for i in range(2)]
        up_bank = [pb(f"up_bank{i}") for i in range(2)]
        y_bank = [pb(f"y_bank{i}") for i in range(2)]
        turn_bank = pb("turn_bank")
        gate_full = sem("gate_full")
        up_full = sem("up_full")
        silu_done = sem("silu_done")
        hidden_done = sem("hidden_done")
        hi_done = sem("hi_done")
        lo_done = sem("lo_done")
        chunk_done = sem("chunk_done")
        y_copied = sem("y_copied")
        y_turned = sem("y_turned")
        added = sem("added")
        sc_full = sem("sc_full")
        sc_copied = sem("sc_copied")
        sc_turned = sem("sc_turned")
        sc_read = sem("sc_read")
        compared = sem("compared")
        weight_done = sem("weight_done")
        stored = sem("stored")
        block = ctx.enter_context(nc.Block())

        def lagging(b, c, lag):
            return (b, c - lag) if c >= lag else (b - 1, c - lag + EC)

        @block.tensor
        def _(pe):
            def turn(b, e):
                pe.wait_ge(y_copied, b * NE + e + 1)
                wait(pe, added, b * NE + e)
                if e == 0:
                    pe.wait_ge(sc_read, b + 1)
                if e == 1 and out is None:
                    wait(pe, n.lo_done, b)
                for t in range(QT):
                    last = nc.tensor.transpose(turn_bank[:, t * P:t * P + P], y_sb[:, t * P:t * P + P], g.ident[:])
                last.then_inc(y_turned, 1)

            def body(b):
                for c in range(EC):
                    m = b * EC + c
                    e, k = divmod(c, NC)
                    if live(b):
                        mv = [x[:, tokens(b)] for x in (g.xn_hi, g.xn_lo)]
                        cols = slice(e * EH + k * P, e * EH + k * P + P)
                        wait(pe, silu_done, m - 1)
                        three_passes(nc, gate_bank[c % 2][:], [w[:, cols] for w in g.w1], mv, True,
                                     True).then_inc(gate_full, 1)
                        wait(pe, hidden_done, m - 1)
                        three_passes(nc, up_bank[c % 2][:], [w[:, cols] for w in g.w2], mv, True,
                                     True).then_inc(up_full, 1)
                        if c == 4:
                            wait(pe, added, b * NE)
                            three_passes(nc, turn_bank[:], [w[:] for w in g.wg], mv, True,
                                         True).then_inc(sc_full, 1)
                        if c == 5:
                            pe.wait_ge(sc_copied, b + 1)
                            for t in range(QT):
                                last = nc.tensor.transpose(turn_bank[:, t * P:t * P + P],
                                                           scores_t[:, t * P:t * P + P], g.ident[:])
                            last.then_inc(sc_turned, 1)
                    if out is None and c == 8 and live(b - 1):
                        pe.wait_ge(added, b * NE + (1 if live(b) else 0))
                        norm_transpose(nc, pe, g, n, b - 1, turn_bank)
                    b6, c6 = lagging(b, c, 6)
                    if c6 % NC == 0 and live(b6):
                        turn(b6, c6 // NC)
                    b2, c2 = lagging(b, c, 2)
                    if live(b2):
                        e2, k2 = divmod(c2, NC)
                        pe.wait_ge(lo_done, m - 1)
                        if k2 == 0:
                            wait(pe, y_copied, b2 * NE + e2 - 1)
                        rows = LAST if k2 == NC - 1 else P
                        st = [w[0:rows, c2 * P:c2 * P + P] for w in g.w3]
                        mv2 = [h[0:rows, :] for h in hidden_parts[c2 % 3]]
                        three_passes(nc, y_bank[e2 % 2][:], st, mv2, k2 == 0, k2 == NC - 1).then_inc(chunk_done, 1)

            each_sequence(pe, body)

        @block.scalar
        def _(act):
            def body(b):
                for c in range(EC):
                    m = b * EC + c
                    if live(b):
                        act.wait_ge(gate_full, m + 1)
                        wait(act, hidden_done, m - 1)
                        nc.scalar.activation(act_gate[c % 2][:], gate_bank[c % 2][:], ACT.Silu).then_inc(silu_done, 1)
                        if c == 4:
                            act.wait_ge(sc_full, b + 1)
                            nc.scalar.activation(scores_t[:], turn_bank[:], ACT.Copy).then_inc(sc_copied, 1)
                    b1, c1 = lagging(b, c, 1)
                    if live(b1):
                        act.wait_ge(hidden_done, m)
                        wait(act, chunk_done, m - 3)
                        nc.scalar.activation(hidden_parts[c1 % 3][0][:], hidden[c1 % 2][:],
                                             ACT.Copy).then_inc(hi_done, 1)
                    b5, c5 = lagging(b, c, 5)
                    if c5 % NC == 0 and live(b5):
                        e5 = c5 // NC
                        act.wait_ge(chunk_done, b5 * EC + c5 + NC)
                        wait(act, y_turned, b5 * NE + e5)
                        nc.scalar.activation(y_sb[:], y_bank[e5 % 2][:], ACT.Copy).then_inc(y_copied, 1)
                    if out is None and c == 8 and live(b - 1):
                        norm_hi(nc, act, g, n, b - 1, turn_bank)

            each_sequence(act, body)

        @block.vector
        def _(dve):
            def add(b, e):
                dve.wait_ge(y_turned, b * NE + e + 1)
                if e == 0:
                    dve.wait_ge(weight_done, b + 1)
                wait(dve, added, b * NE + e)
                for t in range(QT):
                    rows = g.x_tok[:, tile(b, t), :]
                    last = nc.vector.scalar_tensor_tensor(rows, turn_bank[:, t * P:t * P + P],
                                                          weight[:, t * NE + e:t * NE + e + 1], rows,
                                                          ALU.mult, ALU.add)
                last.then_inc(added, 1)

            def rank_experts(b):
                dve.wait_ge(sc_turned, b + 1)
                nc.vector.tensor_copy(scores[:].rearrange("p (t e) -> p t e", t=QT),
                                      turn_bank[:].rearrange("p (t e) -> p t e", t=QT)[:, :, 0:NE]).then_inc(sc_read, 1)
                dve.wait_ge(sc_read, b + 1)
                other = scores[:].rearrange("p (t j) -> p t j", t=QT).unsqueeze(2).to_broadcast([P, QT, NE, NE])
                this = scores[:].rearrange("p (t e) -> p t e", t=QT).unsqueeze(3).to_broadcast([P, QT, NE, NE])
                by4 = lambda a: a[:].rearrange("p (t e) j -> p t e j", t=QT)
                nc.vector.tensor_tensor(by4(better), other, this, ALU.is_gt).then_inc(compared, 1)
                nc.vector.tensor_tensor(by4(equal), other, this, ALU.is_equal).then_inc(compared, 1)
                dve.wait_ge(compared, b * 5 + 2)
                nc.vector.tensor_tensor(by4(equal), by4(equal),
                                        g.earlier[:].unsqueeze(1).to_broadcast([P, QT, NE, NE]),
                                        ALU.mult).then_inc(compared, 1)
                dve.wait_ge(compared, b * 5 + 3)
                nc.vector.tensor_tensor(better[:], better[:], equal[:], ALU.add).then_inc(compared, 1)
                dve.wait_ge(compared, b * 5 + 4)
                nc.vector.tensor_reduce(rank[:], better[:], AX.X, ALU.add).then_inc(compared, 1)
                dve.wait_ge(compared, b * 5 + 5)
                nc.vector.scalar_tensor_tensor(weight[:], rank[:], 2.0, scores[:], ALU.is_lt,
                                               ALU.mult).then_inc(weight_done, 1)

            def body(b):
                for c in range(EC):
                    m = b * EC + c
                    if live(b):
                        dve.wait_ge(up_full, m + 1)
                        dve.wait_ge(silu_done, m + 1)
                        wait(dve, lo_done, m - 1)
                        nc.vector.tensor_tensor(hidden[c % 2][:], act_gate[c % 2][:], up_bank[c % 2][:],
                                                ALU.mult).then_inc(hidden_done, 1)
                    b1, c1 = lagging(b, c, 1)
                    if live(b1):
                        dve.wait_ge(hi_done, m)
                        hi, lo = hidden_parts[c1 % 3]
                        nc.vector.tensor_tensor(lo[:], hidden[c1 % 2][:], hi[:].bitcast(F32),
                                                ALU.subtract).then_inc(lo_done, 1)
                    if c == 5 and live(b):
                        rank_experts(b)
                    b6, c6 = lagging(b, c, 6)
                    if c6 % NC == 0 and live(b6):
                        add(b6, c6 // NC)
                    if out is None and live(b - 1):
                        if c == 4:
                            wait_apart(nc, dve, g, added, b * NE)
                            norm_stats(nc, dve, g, n, b - 1)
                        if c == 7:
                            norm_apply(nc, dve, g, n, b - 1)
                        if c == 8:
                            norm_lo(nc, dve, g, n, b - 1, turn_bank)

            each_sequence(dve, body)

        @block.gpsimd
        def _(pool):
            if out is None:
                norm_rstd(nc, pool, g, n, 0)
                with pool.Fori(1, NB) as b:
                    norm_rstd(nc, pool, g, n, b)

        @block.sync
        def _(sp):
            if out is not None:
                with sp.Fori(0, NB) as b:
                    sp.wait_ge(added, b * NE + NE)
                    sp.dma_start(out[bass.ds(b * T, T), :].rearrange("(t p) d -> p t d", p=P),
                                 g.x_tok[:, bass.ds(b * QT, QT), :]).then_inc(stored, 16)
                sp.wait_ge(stored, NB * 16)



def attention_b(nc, g):
    VQ = 4
    VW = QT * VQ * 2 * KD
    NORM = 7
    NORM_BANKS = ((0, 2), (2, 3), (3, 4))
    slots = [NH - 1, *range(NH - 1)]
    turn_at, qk_at, v_at, at = {}, {}, {}, 0
    for h in slots:
        if h % VQ in (0, 1):
            v_at[h // VQ, h % VQ] = at
            at += 1
        if h % 2:
            qk_at[(h + 1) // 2 % NP] = at
            at += 2
        turn_at[h] = at
        at += 3
        if h == NORM:
            norm_at = at
            at += len(NORM_BANKS)
    RB = at
    assert RB % 3 == 0
    with ExitStack() as ctx:
        hd = Head(nc, ctx, "b", g, 2, 2 * VW)
        sb = lambda n, s, d: ctx.enter_context(nc.sbuf_tensor(n, s, d))
        n = Norm(nc, ctx, "n3", hd.z)
        q = (sb("q_hi", [P, T], F32R), sb("q_lo", [P, T], F32R))
        k = (sb("k_hi", [P, T], F32R), sb("k_lo", [P, T], F32R))
        block = ctx.enter_context(nc.Block())

        def entry(step, at):
            if isinstance(step, int) and step == 0:
                return at - sum(3 for gone in (turn_at[NH - 1], turn_at[0], norm_at) if at > gone)
            if isinstance(step, int) and step == NB:
                kept = (turn_at[NH - 1], turn_at[0], norm_at)
                return NB * RB - 9 + sum(min(3, at - k) for k in kept if at > k)
            return step * RB - 9 + at

        def bank_free(pe, step, at):
            wait(pe, hd.ring_lo, entry(step, at) - (0 if isinstance(step, int) and step == NB else 2))

        def v_parts(quarter, i):
            v = hd.v[:, quarter % 2 * VW + i * VW // 2:quarter % 2 * VW + (i + 1) * VW // 2]
            v = v.rearrange("p (h c) -> p h c", c=2 * KD)
            return v[:, :, 0:KD], v[:, :, KD:2 * KD], lambda bank: bank[:].rearrange("p (h c) -> p h c", c=KD)

        def head_at(b, h, lag):
            b, h = (b, h - lag) if h >= lag else (b - 1, h - lag + NH)
            return b, h, b * NH + h

        def pair_at(b, h, lag):
            b, h, _ = head_at(b, h, lag)
            return (b, h // 2) if h % 2 == 0 else (-1, 0)

        def norm_parts(i, b):
            first, end = NORM_BANKS[i]
            cols = bass.ds(b * T + first * P, (end - first) * P)
            return g.xn_hi[:, cols], g.xn_lo[:, cols], lambda bank: bank[:, 0:(end - first) * P]

        @block.sync
        def _(sp):
            load_x_cur(sp, g, hd, 0)
            with sp.Fori(1, NB) as b:
                sp.wait_ge(hd.filled, entry(b - 1, v_at[NH // VQ - 1, 1] + 1))
                load_x_cur(sp, g, hd, b)

        @block.gpsimd
        def _(pool):
            def body(step):
                for h in slots:
                    b = step - 1 if h == NH - 1 else step
                    if live(b - 1) and h == 5:
                        norm_rstd(nc, pool, g, n, b - 1)
                    if live(b):
                        head_probs(nc, pool, hd, b * NH + h, hd.probs[h % 2])

            each_sequence(pool, body)

        @block.tensor
        def _(pe):
            def project(step, h, i):
                if h % 2 == 0 or not live(step):
                    return
                p = (h + 1) // 2 % NP
                at, w = qk_at[p] + i, (g.b_q, g.b_k)[i]
                bank_free(pe, step, at)
                three_passes(nc, hd.ring[at % 3][:], [v[:, p * P:p * P + P] for v in w],
                             [x[:, tokens(step)] for x in (g.xn_hi, g.xn_lo)], True, True).then_inc(hd.filled, 1)

            def values(step, b, h):
                if h % VQ > 1 or not live(b):
                    return
                quarter, i = divmod(h, VQ)
                if h == 0:
                    pe.wait_ge(hd.x_cur_in, b * 32 + 32)
                cols = slice(quarter * VQ * KD, (quarter + 1) * VQ * KD)
                at = v_at[quarter, i]
                bank_free(pe, step, at)
                for j in range(2):
                    t = 2 * i + j
                    last = three_passes(nc, hd.ring[at % 3][:, j * VQ * KD:(j + 1) * VQ * KD],
                                        [x[:, t * P:t * P + P] for x in hd.x_cur],
                                        [v[:, cols] for v in g.b_v], True, True)
                last.then_inc(hd.filled, 1)

            def scores(step, b, h, group):
                if not live(b):
                    return
                if h % 2 == 0 and group == 0:
                    pe.wait_ge(hd.ring_lo, entry(step, qk_at[h // 2] + 2))
                rows = slice(h % 2 * KD, h % 2 * KD + KD)
                s_free(pe, hd, b * NH + h, group)
                for i in S_GROUPS[group]:
                    st = [v[rows, i * P:i * P + P] for v in q]
                    mv = [v[rows, 0:(i + 1) * P] for v in k]
                    three_passes(nc, s_tile(hd, i), st, mv, True, False)
                    last = head_mask(nc, hd, i)
                last.then_inc(hd.s_full, 1)

            def products(step, b, h, u):
                if not live(b):
                    return
                made = entry(step - 1 if h == NH - 3 else step, turn_at[(h + 1) % NH] + 3)
                v0 = h // VQ % 2 * VW + h % VQ * 2 * KD
                head_pv(nc, pe, hd, u, made, lambda j: v0 + j * VQ * 2 * KD)

            def transposes(step, b, h, u, k):
                if live(b):
                    at = turn_at[(h + 1) % NH] + k
                    bank_free(pe, step, at)
                    head_transpose(nc, pe, hd, u, hd.probs[h % 2], k, at)

            def output(b, p):
                if not live(b):
                    return
                pe.wait_ge(hd.y_lo_done, b * NP + p + 1)
                if p == 0:
                    wait(pe, hd.x_done, b)
                three_passes(nc, hd.z_bank[:], [w[:, p * P:p * P + P] for w in g.b_w],
                             [y[:] for y in hd.y_parts], p == 0, p == NP - 1).then_inc(hd.z_full, 1)

            def norm_turned(b):
                pe.wait_ge(n.xn_done, b * QT + QT)
                for k, tiles in enumerate(NORM_BANKS):
                    bank_free(pe, b + 1, norm_at + k)
                    for t in range(*tiles):
                        to = (t - tiles[0]) * P
                        last = nc.tensor.transpose(hd.ring[(norm_at + k) % 3][:, to:to + P],
                                                   n.xn[:, t * D:t * D + D], g.ident[:])
                    last.then_inc(hd.filled, 1)

            def body(step):
                for h in slots:
                    b = step - 1 if h == NH - 1 else step
                    one, two = head_at(b, h, 1), head_at(b, h, 2)
                    scores(step, b, h, 0)
                    scores(step, b, h, 1)
                    if h % VQ == 1:
                        values(step, b, h)
                    project(step, h, 0)
                    scores(step, b, h, 2)
                    if h % VQ == 0:
                        values(step, b, h)
                    project(step, h, 1)
                    products(step, *two)
                    transposes(step, *one, 0)
                    transposes(step, *one, 1)
                    output(*pair_at(b, h, 5))
                    transposes(step, *one, 2)
                    if live(b - 1) and h == 4:
                        output_transpose(nc, pe, hd, b - 1)
                    if live(b - 1) and h == NORM:
                        norm_turned(b - 1)

            each_sequence(pe, body)

        @block.scalar
        def _(act):
            def exponentials(b, h, group):
                if live(b):
                    head_exp(nc, act, hd, b * NH + h, group, hd.probs[h % 2])

            def project_hi(step, b, h, i):
                if h % 2 and live(step):
                    if i == 0 and live(b):
                        act.wait_ge(hd.s_full, (b * NH + h + 1) * len(S_GROUPS))
                    at = qk_at[(h + 1) // 2 % NP] + i
                    split_hi(nc, act, hd, entry(step, at), at, (q, k)[i][0][:])

            def values_hi(step, b, h):
                if live(b):
                    hi, lo, bank = v_parts(*divmod(h, VQ))
                    at = v_at[divmod(h, VQ)]
                    split_hi(nc, act, hd, entry(step, at), at, hi, bank)

            def transposes_hi(step, b, h, k):
                if live(b):
                    at = turn_at[(h + 1) % NH] + k
                    head_transposed_hi(nc, act, hd, entry(step, at), at, k)

            def y_hi(b, p):
                if live(b):
                    act.wait_ge(hd.y_done, b * NH + 2 * p + 2)
                    wait(act, hd.z_full, b * NP + p)
                    nc.scalar.activation(hd.y_parts[0][:], hd.y[:], ACT.Copy).then_inc(hd.y_hi_done, 1)

            def body(step):
                for h in slots:
                    b = step - 1 if h == NH - 1 else step
                    b1, h1, _ = head_at(b, h, 1)
                    b2, h2, u2 = head_at(b, h, 2)
                    exponentials(b, h, 0)
                    project_hi(step, b, h, 0)
                    y_hi(*pair_at(b, h, 4))
                    if h % VQ == 0:
                        values_hi(step, b, h)
                    exponentials(b, h, 1)
                    project_hi(step, b, h, 1)
                    transposes_hi(step, b1, h1, 0)
                    transposes_hi(step, b1, h1, 1)
                    exponentials(b, h, 2)
                    transposes_hi(step, b1, h1, 2)
                    if live(b2):
                        head_low(nc, act, hd, u2, h2 % 2 * KD, b2 * NP + h2 // 2)
                    if live(b - 1) and h == 3:
                        output_copy(nc, act, hd, b * NP)
                    if h % VQ == 0:
                        values_hi(step, b, h + 1)
                    if live(b - 1) and h == NORM:
                        for i in range(3):
                            hi, lo, bank = norm_parts(i, b - 1)
                            split_hi(nc, act, hd, entry(step, norm_at + i), norm_at + i, hi, bank)

            each_sequence(act, body)

        @block.vector
        def _(dve):
            def maxima(b, h, group):
                if live(b):
                    head_max(nc, dve, hd, b * NH + h, group)

            def project_lo(step, h, i):
                if h % 2 and live(step):
                    at = qk_at[(h + 1) // 2 % NP] + i
                    hi, lo = (q, k)[i]
                    split_lo(nc, dve, hd, entry(step, at), at, lo[:], hi[:])

            def values_lo(step, b, h):
                if live(b):
                    hi, lo, bank = v_parts(*divmod(h, VQ))
                    at = v_at[divmod(h, VQ)]
                    split_lo(nc, dve, hd, entry(step, at), at, lo, hi, bank)

            def transposes_lo(step, b, h, k):
                if live(b):
                    at = turn_at[(h + 1) % NH] + k
                    head_transposed_lo(nc, dve, hd, entry(step, at), at, k)

            def y_lo(b, p):
                if live(b):
                    dve.wait_ge(hd.y_hi_done, b * NP + p + 1)
                    nc.vector.tensor_tensor(hd.y_parts[1][:], hd.y[:], hd.y_parts[0][:].bitcast(F32),
                                            ALU.subtract).then_inc(hd.y_lo_done, 1)

            def body(step):
                for h in slots:
                    b = step - 1 if h == NH - 1 else step
                    b1, h1, _ = head_at(b, h, 1)
                    b3, h3, u3 = head_at(b, h, 3)
                    maxima(b, h, 0)
                    if live(b3):
                        head_y(nc, dve, hd, u3, h3 % 2 * KD)
                    maxima(b, h, 1)
                    if h % VQ == 1:
                        values_lo(step, b, h)
                    maxima(b, h, 2)
                    if h % VQ == 0:
                        values_lo(step, b, h)
                    y_lo(*pair_at(b, h, 4))
                    project_lo(step, h, 0)
                    project_lo(step, h, 1)
                    transposes_lo(step, b1, h1, 0)
                    transposes_lo(step, b1, h1, 1)
                    if live(b):
                        head_recip(nc, dve, hd, b * NH + h)
                    transposes_lo(step, b1, h1, 2)
                    if live(b - 1) and h == 4:
                        output_add(nc, dve, g, hd, b - 1)
                        norm_stats(nc, dve, g, n, b - 1)
                    if live(b - 1) and h == 6:
                        norm_apply(nc, dve, g, n, b - 1, xn_free=True)
                    if live(b - 1) and h == NORM:
                        for i in range(3):
                            hi, lo, bank = norm_parts(i, b - 1)
                            split_lo(nc, dve, hd, entry(step, norm_at + i), norm_at + i, lo, hi, bank)

            each_sequence(dve, body)



def build(nc, ins, out):
    g = Shared()
    with ExitStack() as ctx:
        sb = lambda n, s, d: ctx.enter_context(nc.sbuf_tensor(n, s, d))
        pair = lambda n, s: (sb(f"{n}_hi", s, F32R), sb(f"{n}_lo", s, F32R))
        g.x_tok = sb("x_tok", [P, NB * QT, D], F32)
        g.xn_hi, g.xn_lo = pair("xn", [P, NB * T])
        g.w1, g.w2 = pair("w1", [P, EHP]), pair("w2", [P, EHP])
        g.w3 = pair("w3", [P, EC * P])
        g.wg = pair("wg", [P, P])
        g.b_q, g.b_k, g.b_v = (pair(f"b_{c}", [P, NH * KD]) for c in "qkv")
        g.b_w = pair("b_w", [P, NP * P])
        g.ident = sb("ident", [P, P], F32)
        g.ident_bf = sb("ident_bf", [P, P], BF16)
        g.mask = sb("mask", [P, P], BF16)
        g.earlier = sb("earlier", [P, NE, NE], F32)
        g.minus_half = sb("minus_half", [P, QT], F32)
        g.eps = sb("eps", [P, QT], F32)
        g.unused = sb("unused", [P, 1], F32)
        with ExitStack() as first:
            sb1 = lambda n, s: first.enter_context(nc.sbuf_tensor(n, s, F32R))
            pair1 = lambda n, s: (sb1(f"{n}_hi", s), sb1(f"{n}_lo", s))
            g.a_wq, g.a_wk = pair1("a_wq", [P, P]), pair1("a_wk", [P, P])
            g.a_wv1, g.a_wv2 = pair1("a_wv1", [P, KD]), pair1("a_wv2", [KD, D])
            prepare(nc, g, ins)
            attention_a(nc, g)
        experts(nc, g, "f1")
        attention_b(nc, g)
        experts(nc, g, "f2", out)


_INS = ['L0_attn_a_x', 'L0_attn_a_w_q', 'L0_attn_a_w_k', 'L0_attn_a_w_v1', 'L0_attn_a_w_v2', 'L0_attn_b_Q',
        'L0_attn_b_K', 'L0_attn_b_V', 'L0_attn_b_W', 'L0_ffn_Wg', 'L0_ffn_W1', 'L0_ffn_W2', 'L0_ffn_W3']


def kernel(**inputs):
    import numpy as _np
    import concourse.bacc as _bacc
    from concourse import mybir as _mybir
    from concourse.bass_utils import run_bass_kernel_spmd as _run

    nc = _bacc.Bacc("TRN2", target_bir_lowering=False, num_devices=1)
    arrays, args = {}, []
    for name in _INS:
        a = _np.ascontiguousarray(inputs[name])
        arrays[f"in_{name}_dram"] = a
        args.append(nc.dram_tensor(f"in_{name}_dram", a.shape, _mybir.dt.from_np(a.dtype), kind="ExternalInput").ap())
    out = nc.dram_tensor("out_0_dram", (NB * T, D), _mybir.dt.float32, kind="ExternalOutput").ap()
    build(nc, args, out)
    r = _run(nc, [arrays], core_ids=[0])
    return _np.asarray(r.results[0]["out_0_dram"]).reshape(NB, T, D)
```

```python
import concourse.bass as bass
from concourse import mybir
from contextlib import ExitStack

F32 = mybir.dt.float32
F32R = mybir.dt.float32r
BF16 = mybir.dt.bfloat16
ALU = mybir.AluOpType
ACT = mybir.ActivationFunctionType
AX = mybir.AxisListType

P = 128
NB, T, D = 8, 512, 128
QT = T // P
KD = 64
NH = 16
NP = NH // 2
NE, EH = 8, 352
EC = NE * EH // P
EPS = 1e-5
MASKED = -3.0e38

P_AT = [0, 128, 384, 768]
PT_AT = {0: 0, 1: 512, 3: 896, 2: 1024}
PT_BANKS = [((0,), 0, 512), ((1, 3), 512, 512), ((2,), 1024, 256)]
NPT = 1280
S_GROUPS = ((1, 0), (2,), (3,))
S_AT = {1: (0, 0), 0: (0, 2 * P), 2: (1, 0), 3: (2, 0)}
S_READ = (2, 3, 4)


def live(b):
    return not isinstance(b, int) or 0 <= b < NB


def wait(eng, sem, value):
    if not isinstance(value, int) or value > 0:
        eng.wait_ge(sem, value)


def wait_apart(nc, dve, g, sem, value):
    wait(dve, sem, value)
    if not isinstance(value, int):
        nc.vector.memset(g.unused[:], 0.0)


def tokens(b):
    return bass.ds(b * T, T)


def tile(b, t):
    return b * QT + t


def three_passes(nc, out, st, mv, start, stop):
    nc.tensor.matmul(out, st[0], mv[0], start=start, stop=False)
    nc.tensor.matmul(out, st[0], mv[1], start=False, stop=False)
    return nc.tensor.matmul(out, st[1], mv[0], start=False, stop=stop)


class Shared:
    pass


def each_sequence(eng, body):
    body(0)
    body(1)
    with eng.Fori(2, NB) as b:
        body(b)
    body(NB)



class Norm:

    def __init__(self, nc, ctx, name, xn=None):
        sb = lambda n, s, d: ctx.enter_context(nc.sbuf_tensor(f"{name}_{n}", s, d))
        sem = lambda n: ctx.enter_context(nc.semaphore(f"{name}_{n}"))
        self.stats = sb("stats", [P, QT, 6], F32)
        self.mv = sb("mv", [P, QT, 2], F32)
        self.veps = sb("veps", [P, QT], F32)
        self.rstd = sb("rstd", [P, QT], F32)
        self.xn = sb("xn", [P, T], F32) if xn is None else xn
        self.stats_done = sem("stats_done")
        self.mv_done = sem("mv_done")
        self.veps_done = sem("veps_done")
        self.rstd_done = sem("rstd_done")
        self.xn_done = sem("xn_done")
        self.xnt_full = sem("xnt_full")
        self.hi_done = sem("hi_done")
        self.lo_done = sem("lo_done")


def norm_stats(nc, dve, g, n, b):
    for t in range(QT):
        nc.vector.bn_stats(n.stats[:, t, :], g.x_tok[:, tile(b, t), :]).then_inc(n.stats_done, 1)
    wait(dve, n.rstd_done, b)
    wait_apart(nc, dve, g, n.stats_done, b * QT + QT)
    for t in range(QT):
        nc.vector.bn_aggr(n.mv[:, t, :], n.stats[:, t, :]).then_inc(n.mv_done, 1)


def norm_rstd(nc, pool, g, n, b):
    wait(pool, n.xn_done, b * QT)
    pool.wait_ge(n.mv_done, b * QT + QT)
    nc.gpsimd.tensor_tensor(n.veps[:], n.mv[:, :, 1], g.eps[:], ALU.add).then_inc(n.veps_done, 1)
    pool.wait_ge(n.veps_done, b + 1)
    nc.gpsimd.tensor_tensor(n.rstd[:], n.veps[:], g.minus_half[:], ALU.pow).then_inc(n.rstd_done, 1)


def norm_apply(nc, dve, g, n, b, xn_free=False):
    dve.wait_ge(n.rstd_done, b + 1)
    dve.wait_ge(n.mv_done, b * QT + QT)
    if not xn_free:
        wait(dve, n.xnt_full, b)
    for t in range(QT):
        nc.vector.tensor_scalar(n.xn[:, t * D:t * D + D], g.x_tok[:, tile(b, t), :], n.mv[:, t, 0:1], n.rstd[:, t:t + 1],
                                ALU.subtract, ALU.mult).then_inc(n.xn_done, 1)


def norm_transpose(nc, pe, g, n, b, bank):
    pe.wait_ge(n.xn_done, b * QT + QT)
    for t in range(QT):
        last = nc.tensor.transpose(bank[:, t * P:t * P + P], n.xn[:, t * D:t * D + D], g.ident[:])
    last.then_inc(n.xnt_full, 1)


def norm_hi(nc, act, g, n, b, bank):
    act.wait_ge(n.xnt_full, b + 1)
    nc.scalar.activation(g.xn_hi[:, tokens(b)], bank[:], ACT.Copy).then_inc(n.hi_done, 1)


def norm_lo(nc, dve, g, n, b, bank):
    dve.wait_ge(n.hi_done, b + 1)
    nc.vector.tensor_tensor(g.xn_lo[:, tokens(b)], bank[:], g.xn_hi[:, tokens(b)].bitcast(F32),
                            ALU.subtract).then_inc(n.lo_done, 1)



def prepare(nc, g, ins):
    x, w_q, w_k, w_v1, w_v2, Q, K, V, W, Wg, W1, W2, W3 = ins
    with ExitStack() as ctx:
        sb = lambda n, s, d: ctx.enter_context(nc.sbuf_tensor(n, s, d))
        pb = lambda n: ctx.enter_context(nc.psum_tensor(n, [P, 512], F32))
        sem = lambda n: ctx.enter_context(nc.semaphore(n))
        n = Norm(nc, ctx, "n0")
        a_raw = sb("a_raw", [P, 3, P], F32)
        v2_raw = sb("v2_raw", [KD, P], F32)
        wg_raw = sb("wg_raw", [NE, D], F32)
        f_raw = [sb(f"f_raw{i}", [P, EC * P], F32) for i in range(2)]
        w3_raw = f_raw[0]
        qkv_raw = [sb(f"qkv_raw{i}", [P, KD, NH], F32) for i in range(4)]
        w_perm = sb("w_perm", [P, NH * KD], F32)
        norm_bank = [pb(f"norm_bank{i}") for i in range(2)]
        bank = [pb(f"prep_bank{i}") for i in range(4)]
        x_in = [sem(f"x_in{b}") for b in range(NB)]
        a_in = sem("a_in")
        wg_in = sem("wg_in")
        f_in = [sem(f"f_in{i}") for i in range(3)]
        b_in = [sem(f"b_in{i}") for i in range(4)]
        zeroed = sem("zeroed")
        consts = sem("consts")
        direct_hi = sem("direct_hi")
        direct_lo = sem("direct_lo")
        perm_done = sem("perm_done")
        turned = sem("turned")
        turned_hi = sem("turned_hi")
        turned_lo = sem("turned_lo")

        direct = [
            (a_raw[:, 0, :], KD ** -0.5, g.a_wq[0][:], g.a_wq[1][:], a_in, 96),
            (a_raw[:, 1, :], 1.0, g.a_wk[0][:], g.a_wk[1][:], a_in, 96),
            (a_raw[:, 2, 0:KD], 1.0, g.a_wv1[0][:], g.a_wv1[1][:], a_in, 96),
            (v2_raw[:], 1.0, g.a_wv2[0][:], g.a_wv2[1][:], a_in, 96),
        ]
        for i, (parts, scale) in enumerate(((g.b_q, 1.0 / 128), (g.b_k, 1.0), (g.b_v, 1.0))):
            raw = qkv_raw[i][:].rearrange("p q h -> p h q")
            hi, lo = (part[:].rearrange("p (h q) -> p h q", h=NH) for part in parts)
            direct.append((raw, scale, hi, lo, b_in[i], 16))

        groups = [([(wg_raw[:], g.ident[0:NE, 0:NE], NE)], wg_in, 16,
                   g.wg[0][:, 0:NE], g.wg[1][:, 0:NE])]
        for i, parts in enumerate((g.w1, g.w2)):
            for j in range(0, EC, 4):
                m = min(4, EC - j)
                groups.append(([(f_raw[i][:, (j + k) * P:(j + k) * P + P], g.ident[:], P) for k in range(m)], f_in[i], 16,
                               parts[0][:, j * P:(j + m) * P], parts[1][:, j * P:(j + m) * P]))
        for c in range(0, EC, 4):
            m = min(4, EC - c)
            groups.append(([(w3_raw[:, (c + k) * P:(c + k + 1) * P], g.ident[:], P) for k in range(m)], f_in[2], 16,
                           g.w3[0][:, c * P:(c + m) * P], g.w3[1][:, c * P:(c + m) * P]))
        for p in range(0, NP, 4):
            groups.append(([(w_perm[:, (p + k) * P:(p + k) * P + P], g.ident[:], P) for k in range(4)],
                           perm_done, 1, g.b_w[0][:, p * P:(p + 4) * P], g.b_w[1][:, p * P:(p + 4) * P]))

        block = ctx.enter_context(nc.Block())

        @block.sync
        def _(sp):
            for b in range(NB):
                sp.dma_start(g.x_tok[:, b * QT:b * QT + QT, :],
                             x[b].rearrange("(t p) d -> p t d", p=P)).then_inc(x_in[b], 16)
                if b == 0:
                    for k in range(2):
                        sp.dma_start(a_raw[:, 0, k * KD:k * KD + KD], w_q).then_inc(a_in, 16)
                        sp.dma_start(a_raw[:, 1, k * KD:k * KD + KD], w_k).then_inc(a_in, 16)
                    sp.dma_start(a_raw[:, 2, 0:KD], w_v1).then_inc(a_in, 16)
                    sp.dma_start(v2_raw[:], w_v2).then_inc(a_in, 16)
            sp.dma_start(wg_raw[:], Wg).then_inc(wg_in, 16)
            for i, w in enumerate((W1, W2)):
                flat = w.rearrange("e h d -> (e h) d").rearrange("(j p) d -> p j d", p=P)
                sp.dma_start(f_raw[i][:].rearrange("p (j d) -> p j d", d=D), flat).then_inc(f_in[i], 16)
            for i, w in enumerate((Q, K, V)):
                sp.dma_start(qkv_raw[i][:], w.rearrange("q d h -> d q h")).then_inc(b_in[i], 16)
            sp.dma_start(qkv_raw[3][:], W).then_inc(b_in[3], 16)
            sp.wait_ge(turned, 7)
            sp.dma_start(w3_raw[:].rearrange("p (e h) -> p e h", e=NE),
                         W3.rearrange("e d h -> d e h")).then_inc(f_in[2], 16)

        @block.gpsimd
        def _(pool):
            nc.gpsimd.memset(g.ident[:], 0.0).then_inc(zeroed, 1)
            nc.gpsimd.memset(g.ident_bf[:], 0.0).then_inc(zeroed, 1)
            nc.gpsimd.memset(g.mask[:], 0.0).then_inc(zeroed, 1)
            nc.gpsimd.memset(g.earlier[:], 0.0).then_inc(zeroed, 1)
            nc.gpsimd.memset(g.minus_half[:], -0.5).then_inc(consts, 1)
            nc.gpsimd.memset(g.eps[:], EPS).then_inc(consts, 1)
            for part in g.wg:
                nc.gpsimd.memset(part[:].bitcast(F32), 0.0).then_inc(consts, 1)
            pool.wait_ge(zeroed, 4)
            for idn in (g.ident, g.ident_bf):
                nc.gpsimd.affine_select(out=idn[:], in_=idn[:], compare_op=ALU.not_equal, fill=1.0, base=0,
                                        pattern=[[-1, P]], channel_multiplier=1).then_inc(consts, 1)
            nc.gpsimd.affine_select(out=g.mask[:].rearrange("p (n k) -> p n k", n=2),
                                    in_=g.mask[:].rearrange("p (n k) -> p n k", n=2), compare_op=ALU.is_ge,
                                    fill=MASKED, base=0, pattern=[[0, 2], [-1, P]],
                                    channel_multiplier=1).then_inc(consts, 1)
            nc.gpsimd.affine_select(out=g.earlier[:], in_=g.earlier[:], compare_op=ALU.is_ge, fill=1.0, base=0,
                                    pattern=[[-1, NE], [1, NE]], channel_multiplier=0).then_inc(consts, 1)
            pool.wait_ge(consts, 8)
            norm_rstd(nc, pool, g, n, 0)
            with pool.Fori(1, NB) as b:
                norm_rstd(nc, pool, g, n, b)

        @block.vector
        def _(dve):
            dve.wait_ge(consts, 8)
            for i in range(4):
                raw, scale, hi, lo, loaded, count = direct[i]
                dve.wait_ge(direct_hi, i + 1)
                nc.vector.scalar_tensor_tensor(lo, raw, scale, hi.bitcast(F32), ALU.mult,
                                               ALU.subtract).then_inc(direct_lo, 1)
            dve.wait_ge(x_in[0], 16)
            norm_stats(nc, dve, g, n, 0)
            norm_apply(nc, dve, g, n, 0)
            for b in range(1, NB):
                dve.wait_ge(x_in[b], 16)
            with dve.Fori(1, NB) as b:
                norm_stats(nc, dve, g, n, b)
                norm_lo(nc, dve, g, n, b - 1, norm_bank[0])
                norm_apply(nc, dve, g, n, b)
            norm_lo(nc, dve, g, n, NB - 1, norm_bank[0])
            dve.wait_ge(b_in[3], 16)
            nc.vector.tensor_scalar(w_perm[:].rearrange("p (h v) -> p h v", h=NH), qkv_raw[3][:].rearrange("p v h -> p h v"), 1.0 / NH, None,
                                    ALU.mult).then_inc(perm_done, 1)
            for i in range(4, len(direct)):
                raw, scale, hi, lo, loaded, count = direct[i]
                dve.wait_ge(direct_hi, i + 1)
                nc.vector.scalar_tensor_tensor(lo, raw, scale, hi.bitcast(F32), ALU.mult,
                                               ALU.subtract).then_inc(direct_lo, 1)
            for i, (tiles, loaded, count, hi, lo) in enumerate(groups):
                dve.wait_ge(turned_hi, i + 1)
                nc.vector.tensor_tensor(lo, bank[i % 4][:, 0:len(tiles) * tiles[0][2]], hi.bitcast(F32),
                                        ALU.subtract).then_inc(turned_lo, 1)

        @block.scalar
        def _(act):
            act.wait_ge(consts, 8)
            for i in range(4):
                raw, scale, hi, lo, loaded, count = direct[i]
                act.wait_ge(loaded, count)
                nc.scalar.activation(hi, raw, ACT.Copy, scale=scale).then_inc(direct_hi, 1)
            with act.Fori(0, NB) as b:
                norm_hi(nc, act, g, n, b, norm_bank[0])
            for i in range(4, len(direct)):
                raw, scale, hi, lo, loaded, count = direct[i]
                act.wait_ge(loaded, count)
                nc.scalar.activation(hi, raw, ACT.Copy, scale=scale).then_inc(direct_hi, 1)
            for i, (tiles, loaded, count, hi, lo) in enumerate(groups):
                act.wait_ge(turned, i + 1)
                nc.scalar.activation(hi, bank[i % 4][:, 0:len(tiles) * tiles[0][2]], ACT.Copy).then_inc(turned_hi, 1)

        @block.tensor
        def _(pe):
            pe.wait_ge(consts, 8)
            norm_transpose(nc, pe, g, n, 0, norm_bank[0])
            with pe.Fori(1, NB) as b:
                pe.wait_ge(n.lo_done, b)
                norm_transpose(nc, pe, g, n, b, norm_bank[0])
            for i, (tiles, loaded, count, hi, lo) in enumerate(groups):
                pe.wait_ge(loaded, count)
                wait(pe, turned_lo, i - 3)
                for k, (src, ident, width) in enumerate(tiles):
                    last = nc.tensor.transpose(bank[i % 4][:, k * width:k * width + width], src, ident)
                last.then_inc(turned, 1)



class Head:

    def __init__(self, nc, ctx, name, g, probs, v_cols):
        sb = lambda n, s, d: ctx.enter_context(nc.sbuf_tensor(f"{name}_{n}", s, d))
        pb = lambda n: ctx.enter_context(nc.psum_tensor(f"{name}_{n}", [P, 512], F32))
        sem = lambda n: ctx.enter_context(nc.semaphore(f"{name}_{n}"))
        self.ident, self.ident_bf, self.mask = g.ident, g.ident_bf, g.mask
        self.probs = [sb(f"probs{i}", [P, NPT], F32) for i in range(probs)]
        self.pt = (sb("pt_hi", [P, NPT], F32R), sb("pt_lo", [P, NPT], F32R))
        self.neg_max = sb("neg_max", [P, QT], F32)
        self.sums = sb("sums", [P, QT], F32)
        self.recip = sb("recip", [P, QT], F32)
        self.v = sb("v", [P, v_cols], F32R)
        self.y = sb("y", [P, T], F32)
        self.y_parts = (sb("y_hi", [P, T], F32R), sb("y_lo", [P, T], F32R))
        self.z = sb("z", [P, T], F32)
        self.x_cur = (sb("x_cur_hi", [P, T], F32R), sb("x_cur_lo", [P, T], F32R))
        self.s_bank = [pb(f"s_bank{i}") for i in range(len(S_GROUPS))]
        self.ring = [pb(f"ring{i}") for i in range(3)]
        self.pv_bank = pb("pv_bank")
        self.z_bank = pb("z_bank")
        self.filled = sem("filled")
        self.ring_hi = sem("ring_hi")
        self.ring_lo = sem("ring_lo")
        self.s_full = sem("s_full")
        self.max_done = sem("max_done")
        self.exp_done = sem("exp_done")
        self.recip_done = sem("recip_done")
        self.probs_done = sem("probs_done")
        self.pv_full = sem("pv_full")
        self.low_done = sem("low_done")
        self.y_done = sem("y_done")
        self.y_hi_done = sem("y_hi_done")
        self.y_lo_done = sem("y_lo_done")
        self.z_full = sem("z_full")
        self.z_done = sem("z_done")
        self.zt_full = sem("zt_full")
        self.x_done = sem("x_done")
        self.x_cur_in = sem("x_cur_in")


def split_hi(nc, act, hd, r, n, dst, src=lambda bank: bank[:]):
    act.wait_ge(hd.filled, r + 1)
    nc.scalar.activation(dst, src(hd.ring[n % 3]), ACT.Copy).then_inc(hd.ring_hi, 1)


def split_lo(nc, dve, hd, r, n, dst, hi, src=lambda bank: bank[:]):
    dve.wait_ge(hd.ring_hi, r + 1)
    nc.vector.tensor_tensor(dst, src(hd.ring[n % 3]), hi.bitcast(F32), ALU.subtract).then_inc(hd.ring_lo, 1)


def head_transpose(nc, pe, hd, u, probs, k, n):
    if k == 0:
        pe.wait_ge(hd.probs_done, u * QT + QT)
    key_tiles, at, width = PT_BANKS[k]
    for j in key_tiles:
        for i in range(j, QT):
            to = PT_AT[j] - at + (i - j) * P
            last = nc.tensor.transpose(hd.ring[n % 3][:, to:to + P],
                                       probs[:, P_AT[i] + j * P:P_AT[i] + j * P + P], hd.ident[:])
    last.then_inc(hd.filled, 1)


def head_transposed_hi(nc, act, hd, r, n, k):
    _, at, width = PT_BANKS[k]
    split_hi(nc, act, hd, r, n, hd.pt[0][:, at:at + width], lambda bank: bank[:, 0:width])


def head_transposed_lo(nc, dve, hd, r, n, k):
    _, at, width = PT_BANKS[k]
    split_lo(nc, dve, hd, r, n, hd.pt[1][:, at:at + width], hd.pt[0][:, at:at + width],
             lambda bank: bank[:, 0:width])


def s_tile(hd, i):
    bank, col = S_AT[i]
    return hd.s_bank[bank][:, col:col + (i + 1) * P]


def s_free(pe, hd, u, group):
    wait(pe, hd.exp_done, (u - 1) * QT + S_READ[group])


def head_mask(nc, hd, group):
    i, n = S_GROUPS[group][0], len(S_GROUPS[group])
    bank, col = S_AT[i]
    return nc.tensor.matmul(hd.s_bank[bank][:, col + i * P:col + (i + n) * P], hd.ident_bf[:],
                            hd.mask[:, 0:n * P], start=False, stop=True)


def head_max(nc, dve, hd, u, group):
    dve.wait_ge(hd.s_full, u * len(S_GROUPS) + group + 1)
    for i in S_GROUPS[group]:
        nc.vector.tensor_reduce(hd.neg_max[:, i:i + 1], s_tile(hd, i), AX.X, ALU.max,
                                negate=True).then_inc(hd.max_done, 1)


def head_exp(nc, act, hd, u, group, probs):
    if group == 0:
        wait(act, hd.recip_done, u)
    act.wait_ge(hd.max_done, u * QT + S_READ[group])
    for i in S_GROUPS[group]:
        nc.scalar.activation(probs[:, P_AT[i]:P_AT[i] + (i + 1) * P], s_tile(hd, i),
                             ACT.Exp, bias=hd.neg_max[:, i:i + 1],
                             accum_out=hd.sums[:, i:i + 1]).then_inc(hd.exp_done, 1)


def head_recip(nc, dve, hd, u):
    dve.wait_ge(hd.exp_done, u * QT + QT)
    wait(dve, hd.probs_done, u * QT)
    nc.vector.reciprocal(hd.recip[:], hd.sums[:]).then_inc(hd.recip_done, 1)


def head_probs(nc, pool, hd, u, probs):
    pool.wait_ge(hd.recip_done, u + 1)
    for i in range(QT):
        part = probs[:, P_AT[i]:P_AT[i] + (i + 1) * P]
        nc.gpsimd.tensor_tensor(part, part, hd.recip[:, i:i + 1].to_broadcast([P, (i + 1) * P]),
                                ALU.mult).then_inc(hd.probs_done, 1)


def head_pv(nc, pe, hd, u, r_end, v_at):
    pe.wait_ge(hd.ring_lo, r_end)
    wait(pe, hd.y_done, u)
    for j in range(QT):
        v = hd.v[:, v_at(j):v_at(j) + 2 * KD]
        for part in range(2):
            last = nc.tensor.matmul(hd.pv_bank[:, j * P:T], v, hd.pt[part][:, PT_AT[j]:PT_AT[j] + T - j * P],
                                    start=(j == 0 and part == 0), stop=(j == QT - 1 and part == 1))
    last.then_inc(hd.pv_full, 1)


def head_low(nc, act, hd, u, row, split):
    act.wait_ge(hd.pv_full, u + 1)
    wait(act, hd.y_lo_done, split)
    nc.scalar.activation(hd.y[row:row + KD, :], hd.pv_bank[KD:P, :], ACT.Copy).then_inc(hd.low_done, 1)


def head_y(nc, dve, hd, u, row):
    dve.wait_ge(hd.low_done, u + 1)
    y = hd.y[row:row + KD, :]
    nc.vector.tensor_tensor(y, hd.pv_bank[0:KD, :], y, ALU.add).then_inc(hd.y_done, 1)


def output_copy(nc, act, hd, full):
    act.wait_ge(hd.z_full, full)
    nc.scalar.activation(hd.z[:], hd.z_bank[:], ACT.Copy).then_inc(hd.z_done, 1)


def output_transpose(nc, pe, hd, b):
    pe.wait_ge(hd.z_done, b + 1)
    for t in range(QT):
        last = nc.tensor.transpose(hd.z_bank[:, t * P:t * P + P], hd.z[:, t * P:t * P + P], hd.ident[:])
    last.then_inc(hd.zt_full, 1)


def output_add(nc, dve, g, hd, b):
    dve.wait_ge(hd.zt_full, b + 1)
    rows = g.x_tok[:, bass.ds(b * QT, QT), :]
    nc.vector.tensor_tensor(rows, rows, hd.z_bank[:].rearrange("p (t d) -> p t d", t=QT),
                            ALU.add).then_inc(hd.x_done, 1)
    wait_apart(nc, dve, g, hd.x_done, b + 1)


def load_x_cur(sp, g, hd, b):
    for part, src in zip(hd.x_cur, (g.xn_hi, g.xn_lo)):
        sp.dma_start(part[:].bitcast(F32), src[:, tokens(b)].bitcast(F32)).then_inc(hd.x_cur_in, 16)



def attention_a(nc, g):
    RA = 6
    with ExitStack() as ctx:
        hd = Head(nc, ctx, "a", g, 1, QT * 2 * KD)
        sb = lambda n, s, d: ctx.enter_context(nc.sbuf_tensor(n, s, d))
        n = Norm(nc, ctx, "n1", hd.z)
        q_stack = sb("q_stack", [P, T], F32R)
        k_twice = (sb("k_twice_hi", [P, T], F32R), sb("k_twice_lo", [P, T], F32R))
        v_parts = [hd.v[:].rearrange("p (t v) -> p t v", t=QT)[:, :, k * KD:k * KD + KD] for k in range(2)]
        v_bank = lambda bank: bank[:, 0:QT * KD].rearrange("p (t v) -> p t v", t=QT)
        block = ctx.enter_context(nc.Block())

        def steps(eng, body):
            for b in range(-1, 4):
                body(b)
            with eng.Fori(4, NB - 1) as b:
                body(b)
            for b in range(NB - 1, NB + 3):
                body(b)

        def qk_at(b, i):
            return (b - 1) * RA + 2 + i if not isinstance(b, int) or b else i, (2 + i) % 3 if not isinstance(b, int) or b else i

        def head_entry(b, i):
            if isinstance(b, int) and b == NB - 1:
                return b * RA + 2 + i, (2 + i) % 3
            return b * RA + 4 + i, (4 + i) % 3

        @block.sync
        def _(sp):
            load_x_cur(sp, g, hd, 0)
            with sp.Fori(1, NB) as b:
                sp.wait_ge(hd.filled, head_entry(b - 1, 0)[0] + 1)
                load_x_cur(sp, g, hd, b)

        @block.gpsimd
        def _(pool):
            def body(b):
                if live(b):
                    head_probs(nc, pool, hd, b, hd.probs[0])
                if live(b - 2):
                    norm_rstd(nc, pool, g, n, b - 2)

            steps(pool, body)

        @block.tensor
        def _(pe):
            def body(b):
                if live(b):
                    pe.wait_ge(hd.ring_lo, qk_at(b, 1)[0] + 1)
                    for group, tiles in enumerate(S_GROUPS):
                        s_free(pe, hd, b, group)
                        for i in tiles:
                            for part in range(2):
                                nc.tensor.matmul(s_tile(hd, i), q_stack[:, i * P:i * P + P],
                                                 k_twice[part][:, 0:(i + 1) * P],
                                                 start=(i == tiles[0] and part == 0), stop=False)
                        head_mask(nc, hd, group).then_inc(hd.s_full, 1)
                if live(b - 3):
                    norm_transpose(nc, pe, g, n, b - 3, hd.z_bank)
                if live(b + 1):
                    for i, w in enumerate((g.a_wq, g.a_wk)):
                        r, bank = qk_at(b + 1, i)
                        wait(pe, hd.ring_lo, r - 2)
                        three_passes(nc, hd.ring[bank][:], [w[0][:], w[1][:]],
                                     [x[:, tokens(b + 1)] for x in (g.xn_hi, g.xn_lo)], True,
                                     True).then_inc(hd.filled, 1)
                if live(b - 1):
                    head_pv(nc, pe, hd, b - 1, head_entry(b - 1, 3)[0] + 1, lambda j: j * 2 * KD)
                if live(b - 2):
                    pe.wait_ge(hd.y_lo_done, b - 1)
                    wait(pe, n.lo_done, b - 2)
                    three_passes(nc, hd.z_bank[:], [w[:] for w in g.a_wv2], [y[0:KD, :] for y in hd.y_parts],
                                 True, True).then_inc(hd.z_full, 1)
                if live(b):
                    r, bank = head_entry(b, 0)
                    pe.wait_ge(hd.ring_lo, r - 2)
                    pe.wait_ge(hd.x_cur_in, b * 32 + 32)
                    for t in range(QT):
                        last = three_passes(nc, hd.ring[bank][:, t * KD:t * KD + KD],
                                            [x[:, t * P:t * P + P] for x in hd.x_cur],
                                            [g.a_wv1[0][:], g.a_wv1[1][:]], True, True)
                    last.then_inc(hd.filled, 1)
                if live(b - 2):
                    output_transpose(nc, pe, hd, b - 2)
                if live(b):
                    for k in range(3):
                        r, bank = head_entry(b, 1 + k)
                        wait(pe, hd.ring_lo, r - 2)
                        head_transpose(nc, pe, hd, b, hd.probs[0], k, bank)

            steps(pe, body)

        @block.scalar
        def _(act):
            def body(b):
                if live(b):
                    head_exp(nc, act, hd, b, 0, hd.probs[0])
                    head_exp(nc, act, hd, b, 1, hd.probs[0])
                if live(b - 3):
                    norm_hi(nc, act, g, n, b - 3, hd.z_bank)
                if live(b):
                    head_exp(nc, act, hd, b, 2, hd.probs[0])
                if live(b + 1):
                    split_hi(nc, act, hd, *qk_at(b + 1, 0), q_stack[:])
                    split_hi(nc, act, hd, *qk_at(b + 1, 1), k_twice[0][:])
                if live(b - 1):
                    head_low(nc, act, hd, b - 1, 0, b - 1)
                if live(b - 2):
                    output_copy(nc, act, hd, b - 1)
                if live(b):
                    split_hi(nc, act, hd, *head_entry(b, 0), v_parts[0], v_bank)
                if live(b - 1):
                    act.wait_ge(hd.y_done, b)
                    wait(act, hd.z_full, b - 1)
                    nc.scalar.activation(hd.y_parts[0][0:KD, :], hd.y[0:KD, :], ACT.Copy).then_inc(hd.y_hi_done, 1)
                if live(b):
                    for k in range(3):
                        head_transposed_hi(nc, act, hd, *head_entry(b, 1 + k), k)

            steps(act, body)

        @block.vector
        def _(dve):
            def body(b):
                if live(b):
                    for group in range(len(S_GROUPS)):
                        head_max(nc, dve, hd, b, group)
                if live(b - 3):
                    norm_lo(nc, dve, g, n, b - 3, hd.z_bank)
                if live(b):
                    head_recip(nc, dve, hd, b)
                if live(b + 1):
                    r, bank = qk_at(b + 1, 0)
                    dve.wait_ge(hd.ring_hi, r + 1)
                    nc.vector.tensor_tensor(q_stack[KD:P, :], hd.ring[bank][KD:P, :], q_stack[KD:P, :].bitcast(F32),
                                            ALU.subtract).then_inc(hd.ring_lo, 1)
                    split_lo(nc, dve, hd, *qk_at(b + 1, 1), k_twice[1][:], k_twice[0][:])
                if live(b - 1):
                    head_y(nc, dve, hd, b - 1, 0)
                if live(b):
                    split_lo(nc, dve, hd, *head_entry(b, 0), v_parts[1], v_parts[0], v_bank)
                if live(b - 2):
                    output_add(nc, dve, g, hd, b - 2)
                if live(b - 1):
                    dve.wait_ge(hd.y_hi_done, b)
                    nc.vector.tensor_tensor(hd.y_parts[1][0:KD, :], hd.y[0:KD, :], hd.y_parts[0][0:KD, :].bitcast(F32),
                                            ALU.subtract).then_inc(hd.y_lo_done, 1)
                if live(b - 2):
                    norm_stats(nc, dve, g, n, b - 2)
                if live(b):
                    for k in range(3):
                        head_transposed_lo(nc, dve, hd, *head_entry(b, 1 + k), k)
                if live(b - 2):
                    norm_apply(nc, dve, g, n, b - 2)

            steps(dve, body)



def experts(nc, g, name, out=None):
    HALF = EC // 2
    slots = [*range(HALF, EC), *range(HALF)]
    spans = [[(e, max(e * EH - c * P, 0), min((e + 1) * EH - c * P, P)) for e in range(NE)
              if e * EH < (c + 1) * P and (e + 1) * EH > c * P] for c in range(EC)]
    tiles = [span for i, span in enumerate(spans) if span not in spans[:i]]
    tile_of = [tiles.index(span) for span in spans]
    last_of = [max(c for c in range(EC) if tile_of[c] == i) for i in range(len(tiles))]
    part_of = [c % 3 for c in range(EC - 1)] + [3]
    with ExitStack() as ctx:
        sb = lambda n, s, d: ctx.enter_context(nc.sbuf_tensor(f"{name}_{n}", s, d))
        pb = lambda n: ctx.enter_context(nc.psum_tensor(f"{name}_{n}", [P, 512], F32))
        sem = lambda n: ctx.enter_context(nc.semaphore(f"{name}_{n}"))
        y_sb = sb("y_sb", [P, T], F32)
        n = Norm(nc, ctx, f"{name}_n", y_sb)
        act_gate = [sb(f"act_gate{i}", [P, T], F32) for i in range(2)]
        hidden = [sb(f"hidden{i}", [P, T], F32) for i in range(2)]
        hidden_parts = [(sb(f"hidden_hi{i}", [P, T], F32R), sb(f"hidden_lo{i}", [P, T], F32R)) for i in range(4)]
        scores_t = sb("scores_t", [P, T], F32)
        scores = sb("scores", [P, QT * NE], F32)
        better = sb("better", [P, QT * NE, NE], F32)
        equal = sb("equal", [P, QT * NE, NE], F32)
        rank = sb("rank", [P, QT * NE], F32)
        weight = sb("weight", [P, QT * NE], F32)
        weight_t = sb("weight_t", [QT * NE, P], F32)
        weight_all = sb("weight_all", [P, len(tiles), QT, P], F32)
        weight_dram = nc.dram_tensor(f"{name}_weight_dram", (NB * QT * NE, P), F32, kind="Internal").ap()
        gate_bank = [pb(f"gate_bank{i}") for i in range(2)]
        up_bank = [pb(f"up_bank{i}") for i in range(2)]
        y_bank = pb("y_bank")
        turn_bank = pb("turn_bank")
        score_bank = pb("score_bank")
        gate_full = sem("gate_full")
        up_full = sem("up_full")
        silu_done = sem("silu_done")
        weighted = sem("weighted")
        hidden_done = sem("hidden_done")
        hi_done = sem("hi_done")
        lo_done = sem("lo_done")
        chunk_done = sem("chunk_done")
        y_copied = sem("y_copied")
        y_turned = sem("y_turned")
        added = sem("added")
        sc_full = sem("sc_full")
        sc_copied = sem("sc_copied")
        sc_turned = sem("sc_turned")
        compared = sem("compared")
        weight_done = sem("weight_done")
        wt_turned = sem("wt_turned")
        wt_copied = sem("wt_copied")
        wt_stored = sem("wt_stored")
        w_in = [sem(f"w_in{i}") for i in range(len(tiles) // 2)]
        stored = sem("stored")
        block = ctx.enter_context(nc.Block())

        def lagging(b, c, lag):
            return (b, c - lag) if c >= lag else (b - 1, c - lag + EC)

        @block.tensor
        def _(pe):
            def weights(step, c):
                if c == HALF:
                    wait(pe, wt_copied, step)
                    three_passes(nc, score_bank[:], [w[:] for w in g.wg],
                                 [x[:, tokens(step)] for x in (g.xn_hi, g.xn_lo)], True, True).then_inc(sc_full, 1)
                if c == HALF + 1:
                    pe.wait_ge(sc_copied, step + 1)
                    for t in range(QT):
                        last = nc.tensor.transpose(score_bank[:, t * P:t * P + P], scores_t[:, t * P:t * P + P],
                                                   g.ident[:])
                    last.then_inc(sc_turned, 1)
                if c == HALF + 7:
                    pe.wait_ge(weight_done, step + 1)
                    nc.tensor.transpose(score_bank[0:QT * NE, 0:P], weight[:], g.ident[:]).then_inc(wt_turned, 1)

            def body(step):
                for c in slots:
                    b = step - 1 if c >= HALF else step
                    m = b * EC + c
                    if live(b):
                        mv = [x[:, tokens(b)] for x in (g.xn_hi, g.xn_lo)]
                        cols = slice(c * P, c * P + P)
                        wait(pe, silu_done, m - 1)
                        three_passes(nc, gate_bank[c % 2][:], [w[:, cols] for w in g.w1], mv, True,
                                     True).then_inc(gate_full, 1)
                        wait(pe, hidden_done, m - 1)
                        three_passes(nc, up_bank[c % 2][:], [w[:, cols] for w in g.w2], mv, True,
                                     True).then_inc(up_full, 1)
                    if live(step):
                        weights(step, c)
                    if c == 4 and live(b - 1):
                        pe.wait_ge(y_copied, b)
                        if out is None:
                            wait(pe, n.lo_done, b - 1)
                        for t in range(QT):
                            last = nc.tensor.transpose(turn_bank[:, t * P:t * P + P], y_sb[:, t * P:t * P + P], g.ident[:])
                        last.then_inc(y_turned, 1)
                    if out is None and c == 10 and live(b - 1):
                        norm_transpose(nc, pe, g, n, b - 1, turn_bank)
                    b3, c3 = lagging(b, c, 3)
                    if live(b3):
                        pe.wait_ge(lo_done, m - 2)
                        if c3 == 0:
                            wait(pe, y_copied, b3)
                        three_passes(nc, y_bank[:], [w[:, c3 * P:c3 * P + P] for w in g.w3],
                                     [h[:] for h in hidden_parts[part_of[c3]]], c3 == 0,
                                     c3 == EC - 1).then_inc(chunk_done, 1)

            each_sequence(pe, body)

        @block.scalar
        def _(act):
            def body(step):
                for c in slots:
                    b = step - 1 if c >= HALF else step
                    m = b * EC + c
                    if c == 3 and live(b - 1):
                        act.wait_ge(chunk_done, b * EC)
                        wait(act, y_turned, b - 1)
                        nc.scalar.activation(y_sb[:], y_bank[:], ACT.Copy).then_inc(y_copied, 1)
                    if live(b):
                        act.wait_ge(gate_full, m + 1)
                        wait(act, hidden_done, m - 1)
                        nc.scalar.activation(act_gate[c % 2][:], gate_bank[c % 2][:], ACT.Silu).then_inc(silu_done, 1)
                    if c == HALF and live(step):
                        act.wait_ge(sc_full, step + 1)
                        nc.scalar.activation(scores_t[:], score_bank[:], ACT.Copy).then_inc(sc_copied, 1)
                    b1, c1 = lagging(b, c, 1)
                    if live(b1):
                        act.wait_ge(hidden_done, m)
                        wait(act, chunk_done, m - 3)
                        nc.scalar.activation(hidden_parts[part_of[c1]][0][:], hidden[c1 % 2][:],
                                             ACT.Copy).then_inc(hi_done, 1)
                    if c == HALF + 7 and live(step):
                        act.wait_ge(wt_turned, step + 1)
                        wait(act, wt_stored, step * 16)
                        nc.scalar.activation(weight_t[:], score_bank[0:QT * NE, 0:P], ACT.Copy).then_inc(wt_copied, 1)
                    if out is None and c == 10 and live(b - 1):
                        norm_hi(nc, act, g, n, b - 1, turn_bank)

            each_sequence(act, body)

        @block.vector
        def _(dve):
            other = scores[:].rearrange("p (t j) -> p t j", t=QT).unsqueeze(2).to_broadcast([P, QT, NE, NE])
            this = scores[:].rearrange("p (t e) -> p t e", t=QT).unsqueeze(3).to_broadcast([P, QT, NE, NE])
            by4 = lambda a: a[:].rearrange("p (t e) j -> p t e j", t=QT)

            def rank_experts(b, stage):
                if stage == 0:
                    dve.wait_ge(sc_turned, b + 1)
                    nc.vector.tensor_copy(scores[:].rearrange("p (t e) -> p t e", t=QT),
                                          score_bank[:].rearrange("p (t e) -> p t e", t=QT)[:, :, 0:NE]).then_inc(compared, 1)
                if stage == 1:
                    dve.wait_ge(compared, b * 6 + 1)
                    nc.vector.tensor_tensor(by4(better), other, this, ALU.is_gt).then_inc(compared, 1)
                    nc.vector.tensor_tensor(by4(equal), other, this, ALU.is_equal).then_inc(compared, 1)
                if stage == 2:
                    dve.wait_ge(compared, b * 6 + 3)
                    nc.vector.tensor_tensor(by4(equal), by4(equal),
                                            g.earlier[:].unsqueeze(1).to_broadcast([P, QT, NE, NE]),
                                            ALU.mult).then_inc(compared, 1)
                if stage == 3:
                    dve.wait_ge(compared, b * 6 + 4)
                    nc.vector.tensor_tensor(better[:], better[:], equal[:], ALU.add).then_inc(compared, 1)
                if stage == 4:
                    dve.wait_ge(compared, b * 6 + 5)
                    nc.vector.tensor_reduce(rank[:], better[:], AX.X, ALU.add).then_inc(compared, 1)
                    dve.wait_ge(compared, b * 6 + 6)
                    nc.vector.scalar_tensor_tensor(weight[:], rank[:], 2.0, scores[:], ALU.is_lt,
                                                   ALU.mult).then_inc(weight_done, 1)

            def body(step):
                for c in slots:
                    b = step - 1 if c >= HALF else step
                    m = b * EC + c
                    if live(b):
                        dve.wait_ge(up_full, m + 1)
                        dve.wait_ge(weighted, m + 1)
                        wait(dve, lo_done, m - 1)
                        nc.vector.tensor_tensor(hidden[c % 2][:], act_gate[c % 2][:], up_bank[c % 2][:],
                                                ALU.mult).then_inc(hidden_done, 1)
                    b1, c1 = lagging(b, c, 1)
                    if live(b1):
                        dve.wait_ge(hi_done, m)
                        hi, lo = hidden_parts[part_of[c1]]
                        nc.vector.tensor_tensor(lo[:], hidden[c1 % 2][:], hi[:].bitcast(F32),
                                                ALU.subtract).then_inc(lo_done, 1)
                    if HALF < c <= HALF + 5 and live(step):
                        rank_experts(step, c - HALF - 1)
                    if c == 4 and live(b - 1):
                        dve.wait_ge(y_turned, b)
                        rows = g.x_tok[:, bass.ds((b - 1) * QT, QT), :]
                        nc.vector.tensor_tensor(rows, rows, turn_bank[:].rearrange("p (t d) -> p t d", t=QT),
                                                ALU.add).then_inc(added, 1)
                    if out is None and live(b - 1):
                        if c == 5:
                            wait_apart(nc, dve, g, added, b)
                            norm_stats(nc, dve, g, n, b - 1)
                        if c == 8:
                            norm_apply(nc, dve, g, n, b - 1)
                        if c == 10:
                            norm_lo(nc, dve, g, n, b - 1, turn_bank)

            each_sequence(dve, body)

        @block.gpsimd
        def _(pool):
            def body(step):
                for c in slots:
                    b = step - 1 if c >= HALF else step
                    m = b * EC + c
                    i = tile_of[c]
                    if live(b):
                        if tile_of.index(i) == c and i % 2 == 0:
                            count = 16 * (len(tiles[i]) + len(tiles[i + 1]))
                            pool.wait_ge(w_in[i // 2], b * count + count)
                        pool.wait_ge(silu_done, m + 1)
                        nc.gpsimd.tensor_tensor(act_gate[c % 2][:], act_gate[c % 2][:],
                                                weight_all[:, i].rearrange("p t q -> p (t q)"),
                                                ALU.mult).then_inc(weighted, 1)
                    if out is None and c == 6 and live(b - 1):
                        norm_rstd(nc, pool, g, n, b - 1)

            each_sequence(pool, body)

        @block.sync
        def _(sp):
            def body(step):
                if live(step):
                    sp.wait_ge(wt_copied, step + 1)
                    in_dram = weight_dram[bass.ds(step * QT * NE, QT * NE), :]
                    sp.dma_start(in_dram, weight_t[:]).then_inc(wt_stored, 16)
                    sp.wait_ge(wt_stored, step * 16 + 16)
                    for i, span in enumerate(tiles):
                        wait(sp, weighted, (step - 1) * EC + last_of[i] + 1)
                        for e, first, end in span:
                            rows = in_dram.rearrange("(t e) q -> e t q", t=QT)[e]
                            sp.dma_start(weight_all[first:end, i], rows.partition_broadcast(end - first)).then_inc(w_in[i // 2], 16)
                if out is not None and live(step - 1):
                    sp.wait_ge(added, step)
                    sp.dma_start(out[bass.ds((step - 1) * T, T), :].rearrange("(t p) d -> p t d", p=P),
                                 g.x_tok[:, bass.ds((step - 1) * QT, QT), :]).then_inc(stored, 16)

            each_sequence(sp, body)
            if out is not None:
                sp.wait_ge(stored, NB * 16)



def attention_b(nc, g):
    VQ = 4
    VW = QT * VQ * 2 * KD
    NORM = 11
    NORM_BANKS = ((0, 2), (2, 3), (3, 4))
    slots = [NH - 1, *range(NH - 1)]
    turn_at, qk_at, v_at, at = {}, {}, {}, 0
    for h in slots:
        if h % VQ in (0, 1):
            v_at[h // VQ, h % VQ] = at
            at += 1
        if h % 2:
            qk_at[(h + 1) // 2 % NP] = at
            at += 2
        turn_at[h] = at
        at += 3
        if h == NORM:
            norm_at = at
            at += len(NORM_BANKS)
    RB = at
    assert RB % 3 == 0
    with ExitStack() as ctx:
        hd = Head(nc, ctx, "b", g, 2, 2 * VW)
        sb = lambda n, s, d: ctx.enter_context(nc.sbuf_tensor(n, s, d))
        n = Norm(nc, ctx, "n3", hd.z)
        q = (sb("q_hi", [P, T], F32R), sb("q_lo", [P, T], F32R))
        k = (sb("k_hi", [P, T], F32R), sb("k_lo", [P, T], F32R))
        block = ctx.enter_context(nc.Block())

        def entry(step, at):
            if isinstance(step, int) and step == 0:
                return at - sum(3 for gone in (turn_at[NH - 1], turn_at[0], norm_at) if at > gone)
            if isinstance(step, int) and step == NB:
                kept = (turn_at[NH - 1], turn_at[0], norm_at)
                return NB * RB - 9 + sum(min(3, at - k) for k in kept if at > k)
            return step * RB - 9 + at

        def bank_free(pe, step, at):
            wait(pe, hd.ring_lo, entry(step, at) - (0 if isinstance(step, int) and step == NB else 2))

        def v_parts(quarter, i):
            v = hd.v[:, quarter % 2 * VW + i * VW // 2:quarter % 2 * VW + (i + 1) * VW // 2]
            v = v.rearrange("p (h c) -> p h c", c=2 * KD)
            return v[:, :, 0:KD], v[:, :, KD:2 * KD], lambda bank: bank[:].rearrange("p (h c) -> p h c", c=KD)

        def head_at(b, h, lag):
            b, h = (b, h - lag) if h >= lag else (b - 1, h - lag + NH)
            return b, h, b * NH + h

        def pair_at(b, h, lag):
            b, h, _ = head_at(b, h, lag)
            return (b, h // 2) if h % 2 == 0 else (-1, 0)

        def norm_parts(i, b):
            first, end = NORM_BANKS[i]
            cols = bass.ds(b * T + first * P, (end - first) * P)
            return g.xn_hi[:, cols], g.xn_lo[:, cols], lambda bank: bank[:, 0:(end - first) * P]

        @block.sync
        def _(sp):
            load_x_cur(sp, g, hd, 0)
            with sp.Fori(1, NB) as b:
                sp.wait_ge(hd.filled, entry(b - 1, v_at[NH // VQ - 1, 1] + 1))
                load_x_cur(sp, g, hd, b)

        @block.gpsimd
        def _(pool):
            def y_lo(b, p):
                if live(b):
                    pool.wait_ge(hd.y_hi_done, b * NP + p + 1)
                    nc.gpsimd.tensor_tensor(hd.y_parts[1][:], hd.y[:], hd.y_parts[0][:].bitcast(F32),
                                            ALU.subtract).then_inc(hd.y_lo_done, 1)

            def body(step):
                for h in slots:
                    b = step - 1 if h == NH - 1 else step
                    if live(b - 1) and h == 7:
                        norm_rstd(nc, pool, g, n, b - 1)
                    if live(b):
                        head_probs(nc, pool, hd, b * NH + h, hd.probs[h % 2])
                    y_lo(*pair_at(b, h, 3))

            each_sequence(pool, body)

        @block.tensor
        def _(pe):
            def project(step, h, i):
                if h % 2 == 0 or not live(step):
                    return
                p = (h + 1) // 2 % NP
                at, w = qk_at[p] + i, (g.b_q, g.b_k)[i]
                bank_free(pe, step, at)
                three_passes(nc, hd.ring[at % 3][:], [v[:, p * P:p * P + P] for v in w],
                             [x[:, tokens(step)] for x in (g.xn_hi, g.xn_lo)], True, True).then_inc(hd.filled, 1)

            def values(step, b, h):
                if h % VQ > 1 or not live(b):
                    return
                quarter, i = divmod(h, VQ)
                if h == 0:
                    pe.wait_ge(hd.x_cur_in, b * 32 + 32)
                cols = slice(quarter * VQ * KD, (quarter + 1) * VQ * KD)
                at = v_at[quarter, i]
                bank_free(pe, step, at)
                for j in range(2):
                    t = 2 * i + j
                    last = three_passes(nc, hd.ring[at % 3][:, j * VQ * KD:(j + 1) * VQ * KD],
                                        [x[:, t * P:t * P + P] for x in hd.x_cur],
                                        [v[:, cols] for v in g.b_v], True, True)
                last.then_inc(hd.filled, 1)

            def scores(step, b, h, group):
                if not live(b):
                    return
                if h % 2 == 0 and group == 0:
                    pe.wait_ge(hd.ring_lo, entry(step, qk_at[h // 2] + 2))
                rows = slice(h % 2 * KD, h % 2 * KD + KD)
                s_free(pe, hd, b * NH + h, group)
                for i in S_GROUPS[group]:
                    st = [v[rows, i * P:i * P + P] for v in q]
                    mv = [v[rows, 0:(i + 1) * P] for v in k]
                    three_passes(nc, s_tile(hd, i), st, mv, i == S_GROUPS[group][0], False)
                head_mask(nc, hd, group).then_inc(hd.s_full, 1)

            def products(step, b, h, u):
                if not live(b):
                    return
                made = entry(step - 1 if h == NH - 3 else step, turn_at[(h + 1) % NH] + 3)
                v0 = h // VQ % 2 * VW + h % VQ * 2 * KD
                head_pv(nc, pe, hd, u, made, lambda j: v0 + j * VQ * 2 * KD)

            def transposes(step, b, h, u, k):
                if live(b):
                    at = turn_at[(h + 1) % NH] + k
                    bank_free(pe, step, at)
                    head_transpose(nc, pe, hd, u, hd.probs[h % 2], k, at)

            def output(b, p):
                if not live(b):
                    return
                pe.wait_ge(hd.y_lo_done, b * NP + p + 1)
                if p == 0:
                    wait(pe, hd.x_done, b)
                three_passes(nc, hd.z_bank[:], [w[:, p * P:p * P + P] for w in g.b_w],
                             [y[:] for y in hd.y_parts], p == 0, p == NP - 1).then_inc(hd.z_full, 1)

            def norm_turned(b):
                pe.wait_ge(n.xn_done, b * QT + QT)
                for k, tiles in enumerate(NORM_BANKS):
                    bank_free(pe, b + 1, norm_at + k)
                    for t in range(*tiles):
                        to = (t - tiles[0]) * P
                        last = nc.tensor.transpose(hd.ring[(norm_at + k) % 3][:, to:to + P],
                                                   n.xn[:, t * D:t * D + D], g.ident[:])
                    last.then_inc(hd.filled, 1)

            def body(step):
                for h in slots:
                    b = step - 1 if h == NH - 1 else step
                    one, two = head_at(b, h, 1), head_at(b, h, 2)
                    scores(step, b, h, 0)
                    scores(step, b, h, 1)
                    if h % VQ == 0:
                        values(step, b, h)
                    scores(step, b, h, 2)
                    if h % VQ == 1:
                        values(step, b, h)
                    project(step, h, 0)
                    project(step, h, 1)
                    products(step, *two)
                    transposes(step, *one, 0)
                    output(*pair_at(b, h, 5))
                    transposes(step, *one, 1)
                    transposes(step, *one, 2)
                    if live(b - 1) and h == 4:
                        output_transpose(nc, pe, hd, b - 1)
                    if live(b - 1) and h == NORM:
                        norm_turned(b - 1)

            each_sequence(pe, body)

        @block.scalar
        def _(act):
            def exponentials(b, h, group):
                if live(b):
                    head_exp(nc, act, hd, b * NH + h, group, hd.probs[h % 2])

            def project_hi(step, h, i):
                if h % 2 and live(step):
                    at = qk_at[(h + 1) // 2 % NP] + i
                    split_hi(nc, act, hd, entry(step, at), at, (q, k)[i][0][:])

            def values_hi(step, b, h):
                if live(b):
                    hi, lo, bank = v_parts(*divmod(h, VQ))
                    at = v_at[divmod(h, VQ)]
                    split_hi(nc, act, hd, entry(step, at), at, hi, bank)

            def transposes_hi(step, b, h, k):
                if live(b):
                    at = turn_at[(h + 1) % NH] + k
                    head_transposed_hi(nc, act, hd, entry(step, at), at, k)

            def y_hi(b, p):
                if live(b):
                    act.wait_ge(hd.y_done, b * NH + 2 * p + 2)
                    wait(act, hd.z_full, b * NP + p)
                    nc.scalar.activation(hd.y_parts[0][:], hd.y[:], ACT.Copy).then_inc(hd.y_hi_done, 1)

            def body(step):
                for h in slots:
                    b = step - 1 if h == NH - 1 else step
                    b1, h1, _ = head_at(b, h, 1)
                    b2, h2, u2 = head_at(b, h, 2)
                    if h % VQ == 0:
                        values_hi(step, b, h)
                    y_hi(*pair_at(b, h, 4))
                    project_hi(step, h, 0)
                    project_hi(step, h, 1)
                    exponentials(b, h, 0)
                    exponentials(b, h, 1)
                    transposes_hi(step, b1, h1, 0)
                    exponentials(b, h, 2)
                    transposes_hi(step, b1, h1, 1)
                    transposes_hi(step, b1, h1, 2)
                    if live(b2):
                        head_low(nc, act, hd, u2, h2 % 2 * KD, b2 * NP + h2 // 2)
                    if live(b - 1) and h == 3:
                        output_copy(nc, act, hd, b * NP)
                    if h % VQ == 0:
                        values_hi(step, b, h + 1)
                    if live(b - 1) and h == NORM:
                        for i in range(3):
                            hi, lo, bank = norm_parts(i, b - 1)
                            split_hi(nc, act, hd, entry(step, norm_at + i), norm_at + i, hi, bank)

            each_sequence(act, body)

        @block.vector
        def _(dve):
            def maxima(b, h, group):
                if live(b):
                    head_max(nc, dve, hd, b * NH + h, group)

            def project_lo(step, h, i):
                if h % 2 and live(step):
                    at = qk_at[(h + 1) // 2 % NP] + i
                    hi, lo = (q, k)[i]
                    split_lo(nc, dve, hd, entry(step, at), at, lo[:], hi[:])

            def values_lo(step, b, h):
                if live(b):
                    hi, lo, bank = v_parts(*divmod(h, VQ))
                    at = v_at[divmod(h, VQ)]
                    split_lo(nc, dve, hd, entry(step, at), at, lo, hi, bank)

            def transposes_lo(step, b, h, k):
                if live(b):
                    at = turn_at[(h + 1) % NH] + k
                    head_transposed_lo(nc, dve, hd, entry(step, at), at, k)

            def body(step):
                for h in slots:
                    b = step - 1 if h == NH - 1 else step
                    b1, h1, _ = head_at(b, h, 1)
                    b3, h3, u3 = head_at(b, h, 3)
                    if live(b3):
                        head_y(nc, dve, hd, u3, h3 % 2 * KD)
                    maxima(b, h, 0)
                    maxima(b, h, 1)
                    if h % VQ < 2:
                        values_lo(step, b, h)
                    maxima(b, h, 2)
                    if live(b - 1) and h == 5:
                        output_add(nc, dve, g, hd, b - 1)
                    if live(b - 1) and h == 6:
                        norm_stats(nc, dve, g, n, b - 1)
                    if live(b - 1) and h == 10:
                        norm_apply(nc, dve, g, n, b - 1, xn_free=True)
                    project_lo(step, h, 0)
                    project_lo(step, h, 1)
                    transposes_lo(step, b1, h1, 0)
                    if live(b):
                        head_recip(nc, dve, hd, b * NH + h)
                    transposes_lo(step, b1, h1, 1)
                    transposes_lo(step, b1, h1, 2)
                    if live(b - 1) and h == NORM:
                        for i in range(3):
                            hi, lo, bank = norm_parts(i, b - 1)
                            split_lo(nc, dve, hd, entry(step, norm_at + i), norm_at + i, lo, hi, bank)

            each_sequence(dve, body)



def build(nc, ins, out):
    g = Shared()
    with ExitStack() as ctx:
        sb = lambda n, s, d: ctx.enter_context(nc.sbuf_tensor(n, s, d))
        pair = lambda n, s: (sb(f"{n}_hi", s, F32R), sb(f"{n}_lo", s, F32R))
        g.x_tok = sb("x_tok", [P, NB * QT, D], F32)
        g.xn_hi, g.xn_lo = pair("xn", [P, NB * T])
        g.w1, g.w2 = pair("w1", [P, EC * P]), pair("w2", [P, EC * P])
        g.w3 = pair("w3", [P, EC * P])
        g.wg = pair("wg", [P, P])
        g.b_q, g.b_k, g.b_v = (pair(f"b_{c}", [P, NH * KD]) for c in "qkv")
        g.b_w = pair("b_w", [P, NP * P])
        g.ident = sb("ident", [P, P], F32)
        g.ident_bf = sb("ident_bf", [P, P], BF16)
        g.mask = sb("mask", [P, 2 * P], BF16)
        g.earlier = sb("earlier", [P, NE, NE], F32)
        g.minus_half = sb("minus_half", [P, QT], F32)
        g.eps = sb("eps", [P, QT], F32)
        g.unused = sb("unused", [P, 1], F32)
        with ExitStack() as first:
            sb1 = lambda n, s: first.enter_context(nc.sbuf_tensor(n, s, F32R))
            pair1 = lambda n, s: (sb1(f"{n}_hi", s), sb1(f"{n}_lo", s))
            g.a_wq, g.a_wk = pair1("a_wq", [P, P]), pair1("a_wk", [P, P])
            g.a_wv1, g.a_wv2 = pair1("a_wv1", [P, KD]), pair1("a_wv2", [KD, D])
            prepare(nc, g, ins)
            attention_a(nc, g)
        experts(nc, g, "f1")
        attention_b(nc, g)
        experts(nc, g, "f2", out)


_INS = ['L0_attn_a_x', 'L0_attn_a_w_q', 'L0_attn_a_w_k', 'L0_attn_a_w_v1', 'L0_attn_a_w_v2', 'L0_attn_b_Q',
        'L0_attn_b_K', 'L0_attn_b_V', 'L0_attn_b_W', 'L0_ffn_Wg', 'L0_ffn_W1', 'L0_ffn_W2', 'L0_ffn_W3']


def kernel(**inputs):
    import numpy as _np
    import concourse.bacc as _bacc
    from concourse import mybir as _mybir
    from concourse.bass_utils import run_bass_kernel_spmd as _run

    nc = _bacc.Bacc("TRN2", target_bir_lowering=False, num_devices=1)
    arrays, args = {}, []
    for name in _INS:
        a = _np.ascontiguousarray(inputs[name])
        arrays[f"in_{name}_dram"] = a
        args.append(nc.dram_tensor(f"in_{name}_dram", a.shape, _mybir.dt.from_np(a.dtype), kind="ExternalInput").ap())
    out = nc.dram_tensor("out_0_dram", (NB * T, D), _mybir.dt.float32, kind="ExternalOutput").ap()
    build(nc, args, out)
    r = _run(nc, [arrays], core_ids=[0])
    return _np.asarray(r.results[0]["out_0_dram"]).reshape(NB, T, D)
```
